# Optimizing a Trainium2 kernel written in Bass

```python
import numpy as np
import jax
import jax.numpy as jnp

def _softmax(x, axis=-1):
    return jax.nn.softmax(x, axis=axis)

def _gelu(x):
    return jax.nn.gelu(x, approximate=True)

def _silu(x):
    return jax.nn.silu(x)

def _sigmoid(x):
    return jax.nn.sigmoid(x)

def _layernorm(x, axis=-1, eps=1e-05):
    m = jnp.mean(x, axis=axis, keepdims=True)
    v = jnp.var(x, axis=axis, keepdims=True)
    return (x - m) / jnp.sqrt(v + eps)

def _scatter_add(tgt, idx, src, axis=0):
    return tgt.at[idx].add(src)

def _segment_sum(src, seg, n):
    return jax.ops.segment_sum(src, seg, n)
kernel_name = 'mk_prb_d1_jaxref_r8_707253'

def setup_inputs(seed: int=0):
    np.random.seed(seed)
    _w = jnp.asarray

    def _L0_attn_setup():
        import jax, jax.numpy as jnp
        import numpy as np
        HEAD_NUM = 16
        NEG_BIG = 1000000.0
        key = jax.random.key(seed)
        ks = jax.random.split(key, 5)
        E = 128
        B, S = (1, 512)
        x = jax.random.normal(ks[0], (B, S, E), dtype=jnp.float32)
        W1 = jax.random.normal(ks[1], (E, 3 * E), dtype=jnp.float32) * (1.0 / np.sqrt(E))
        b1 = jax.random.normal(ks[2], (3 * E,), dtype=jnp.float32) * 0.02
        Wp = jax.random.normal(ks[3], (E, E), dtype=jnp.float32) * (1.0 / np.sqrt(E))
        bp = jax.random.normal(ks[4], (E,), dtype=jnp.float32) * 0.02
        return {'x': x, 'W1': W1, 'b1': b1, 'Wp': Wp, 'bp': bp}
    _L0_attn_in = _L0_attn_setup()

    def _L0_ffn_setup():
        import jax, jax.numpy as jnp
        import numpy as np
        NUM_EXPERTS = 8
        CAPACITY = 512
        key = jax.random.key(seed)
        ks = jax.random.split(key, 5)
        dim, hidden = (128, 256)
        x = jax.random.normal(ks[0], (4, 512, dim), dtype=jnp.float32)
        wg = jax.random.normal(ks[1], (dim, NUM_EXPERTS), dtype=jnp.float32) * 0.02
        w1 = jax.random.normal(ks[2], (NUM_EXPERTS, dim, hidden), dtype=jnp.float32) * 0.02
        w3 = jax.random.normal(ks[3], (NUM_EXPERTS, dim, hidden), dtype=jnp.float32) * 0.02
        w2 = jax.random.normal(ks[4], (NUM_EXPERTS, hidden, dim), dtype=jnp.float32) * 0.02
        return {'x': x, 'wg': wg, 'w1': w1, 'w3': w3, 'w2': w2}
    _L0_ffn_in = _L0_ffn_setup()
    _d = {'L0_attn_x': _L0_attn_in['x'], 'L0_attn_W1': _L0_attn_in['W1'], 'L0_attn_b1': _L0_attn_in['b1'], 'L0_attn_Wp': _L0_attn_in['Wp'], 'L0_attn_bp': _L0_attn_in['bp'], 'L0_ffn_wg': _L0_ffn_in['wg'], 'L0_ffn_w1': _L0_ffn_in['w1'], 'L0_ffn_w3': _L0_ffn_in['w3'], 'L0_ffn_w2': _L0_ffn_in['w2']}
    _x0 = _d['L0_attn_x']
    _d['L0_attn_x'] = jax.random.normal(jax.random.fold_in(jax.random.key(seed), 1), (8, 256, 128), dtype=_x0.dtype)
    del _x0
    return _d

def reference(L0_attn_x, L0_attn_W1, L0_attn_b1, L0_attn_Wp, L0_attn_bp, L0_ffn_wg, L0_ffn_w1, L0_ffn_w3, L0_ffn_w2):

    def _L0_attn_ref(x, W1, b1, Wp, bp):
        import jax, jax.numpy as jnp
        import numpy as np
        HEAD_NUM = 16
        NEG_BIG = 1000000.0
        B, S, E = x.shape
        H = HEAD_NUM
        d = E // H
        dk = jnp.asarray(d, x.dtype) ** 0.5
        h = x @ W1 + b1
        h = jnp.swapaxes(h.reshape(B, S, H, 3 * d), 1, 2)
        q, k, v = (h[..., :d], h[..., d:2 * d], h[..., 2 * d:])
        w = jnp.einsum('bhqd,bhkd->bhqk', q, k) / dk
        mask = jnp.tril(jnp.ones((S, S), dtype=x.dtype))
        w = jax.nn.softmax(w * mask - (1.0 - mask) * NEG_BIG, axis=-1)
        a = jnp.einsum('bhqk,bhkd->bhqd', w, v)
        a = jnp.swapaxes(a, 1, 2).reshape(B, S, E)
        return a @ Wp + bp

    def _L0_ffn_ref(x, wg, w1, w3, w2):
        import jax, jax.numpy as jnp
        import numpy as np
        NUM_EXPERTS = 8
        CAPACITY = 512
        bz, slen, dim = x.shape
        xt = x.reshape(bz * slen, dim)
        scores = jax.nn.softmax(xt @ wg, axis=-1)
        top_scores, sel = jax.lax.top_k(scores.T, CAPACITY)
        token_idx = sel.reshape(-1)
        routed = xt[token_idx] * top_scores.reshape(-1, 1)
        routed = routed.reshape(NUM_EXPERTS, CAPACITY, dim)
        h = jax.nn.silu(jnp.einsum('ecd,edh->ech', routed, w1)) * jnp.einsum('ecd,edh->ech', routed, w3)
        routed_out = jnp.einsum('ech,ehd->ecd', h, w2).reshape(-1, dim)
        out = jnp.zeros_like(xt).at[token_idx].add(routed_out)
        return out.reshape(bz, slen, dim)
    x = L0_attn_x
    xn = _layernorm(x, axis=-1)
    x = x + _L0_attn_ref(xn, L0_attn_W1, L0_attn_b1, L0_attn_Wp, L0_attn_bp) + _L0_ffn_ref(xn, L0_ffn_wg, L0_ffn_w1, L0_ffn_w3, L0_ffn_w2)
    return x

_drawn_inputs = setup_inputs


def setup_inputs(seed=0):
    import zlib

    import numpy as np

    out = dict(_drawn_inputs(seed))
    spreads = {}
    factors = {'L0_attn_b1': 3.08,
     'L0_attn_bp': 2.847,
     'L0_ffn_wg': 8.0,
     'L0_ffn_w1': 8.0,
     'L0_ffn_w3': 8.0,
     'L0_ffn_w2': 8.0}
    for name, (base, spread) in spreads.items():
        noise = np.random.default_rng([zlib.crc32(name.encode()), seed]).standard_normal(out[name].shape)
        drawn = base * np.exp(spread * noise) if base else spread * noise
        out[name] = jnp.asarray(drawn.astype(out[name].dtype))
    for name, factor in factors.items():
        out[name] = (out[name] * factor).astype(out[name].dtype)
    return out
```

```python
from contextlib import ExitStack

import concourse.bass as bass
from concourse import mybir

ALU = mybir.AluOpType
ACT = mybir.ActivationFunctionType
F32 = mybir.dt.float32
BF16 = mybir.dt.bfloat16
I32 = mybir.dt.int32
U32 = mybir.dt.uint32
AX_X = mybir.AxisListType.X

P = 128
HEADS = 16
TOP_BIT = 29
CAND_START = 1 << TOP_BIT


def attention_moe_block(nc, x, w_qk, b_qk, w_v, b_v, w_p, b_p, w_gate, w1, w3, w2, out):
    B, S, E = x.shape
    NE, _, HID = w1.shape
    TOKENS = B * S
    TILES = TOKENS // P
    CAP = TOKENS // 4
    SLOT_TILES = CAP // P
    HC = HID // P
    D = E // HEADS
    CHUNK = 512
    CT = CHUNK // P
    CHUNKS = TOKENS // CHUNK
    PARTS = 3
    GROUPS = 6
    KS = GROUPS * D
    KM = KS + PARTS
    ROW = E + NE
    INV_SQRT_D = float(D) ** -0.5
    MASKED = -1.0e6
    assert E == P and S == 2 * P and NE == B and HEADS == 16 and CAP == CHUNK and TILES * NE == P

    x_tok = x.rearrange("b (u p) e -> p (b u) e", p=P)
    out_tok = out.rearrange("b (u p) e -> p (b u) e", p=P)

    with ExitStack() as ctx:
        def sb(name, shape, dt=F32):
            return ctx.enter_context(nc.sbuf_tensor(name, shape, dt))

        def bank(name):
            return ctx.enter_context(nc.psum_tensor(name, [P, 512], F32))

        def sem(name):
            return ctx.enter_context(nc.semaphore(name))

        table = nc.dram_tensor("token_table", (TOKENS, ROW), F32).ap()
        acc = nc.dram_tensor("expert_sum", (TOKENS, E), F32).ap()
        qk_dram = nc.dram_tensor("qk_parts", (2, PARTS, 2, P // 2, TOKENS), BF16).ap()

        nat_ps = [bank("nat_ps0"), bank("nat_ps1")]
        tr_ps = [bank("tr_ps0"), bank("tr_ps1")]
        pv_ps = bank("pv_ps")
        ff_ps = [bank("gate_ps"), bank("up_ps")]
        misc_ps = bank("misc_ps")

        ident = sb("ident", [P, P])
        ident16 = sb("ident16", [P, P], BF16)
        causal16 = sb("causal16", [P, 4, P], BF16)
        zero16 = sb("zero16", [P, 4, P], BF16)
        ones = sb("ones", [P, P])
        ones16 = sb("ones16", [P, 1], BF16)
        exp_of_row = sb("exp_of_row", [NE, P], BF16)
        same16 = sb("same16", [P, P], BF16)
        prior16 = sb("prior16", [P, P], BF16)
        sel_exp = sb("sel_exp", [P, NE], BF16)
        slot_row = sb("slot_row", [P, CAP])
        slot_col = sb("slot_col", [P, SLOT_TILES])
        bits_i = sb("bits_i", [P, TOP_BIT + 1], I32)
        bits_f = sb("bits_f", [P, TOP_BIT + 1])
        exponents = sb("exponents", [P, TOP_BIT + 1], I32)

        x_nat = sb("x_nat", [P, TILES, E])
        stats = sb("stats", [P, TILES, 6])
        mean_var = sb("mean_var", [P, TILES, 2])
        rstd = sb("rstd", [P, TILES])
        var_eps = sb("var_eps", [P, TILES])
        neg_half = sb("neg_half", [P, CT])
        xn = sb("xn", [P, TILES, ROW])
        xnT = sb("xnT", [P, TOKENS])
        wqk_sb = sb("wqk_sb", [P, 2, P])
        bqk_sb = sb("bqk_sb", [P, 2])
        wvg_sb = sb("wvg_sb", [P, ROW])
        bv_sb = sb("bv_sb", [P, E])
        bp_sb = sb("bp_sb", [P, E])
        wp_sb = sb("wp_sb", [P, E])
        qk_f = sb("qk_f", [P, 2, CHUNK])
        qk_rest = sb("qk_rest", [P, 2, CHUNK])
        qk_parts = sb("qk_parts_sb", [P, 2, 2, PARTS, CHUNK], BF16)
        v_nat = sb("v_nat", [P, TILES, E])
        x_bias = sb("x_bias", [P, TILES, E])

        logits = sb("logits", [P, TILES, NE])
        row_max = sb("row_max", [P, TILES])
        shifted = sb("shifted", [P, TILES, NE])
        exped = sb("exped", [P, TILES, NE])
        row_sum = sb("row_sum", [P, TILES])
        row_inv = sb("row_inv", [P, TILES])
        scores = sb("scores", [P, TILES, NE])
        scoresT = sb("scoresT", [P, P])
        cmp = sb("cmp", [P, P])
        count = sb("count", [P, 1], BF16)
        cand = sb("cand", [P, 1], I32)
        cand_next = sb("cand_next", [P, 1], I32)
        reject = sb("reject", [P, 1], I32)
        above = sb("above", [P, P])
        equal = sb("equal", [P, P])
        gt_eq = sb("gt_eq", [P, 2])
        gt_eq16 = sb("gt_eq16", [P, 2], BF16)
        need = sb("need", [P, 1])
        eq_prior = sb("eq_prior", [P, 1])
        eq_rank = sb("eq_rank", [P, P])
        eq_in = sb("eq_in", [P, P])
        eq_kept = sb("eq_kept", [P, P])
        chosen = sb("chosen", [P, P])
        rank = sb("rank", [P, P])
        taken16 = sb("taken16", [P, 1], BF16)
        first = sb("first", [P, 1])
        last = sb("last", [P, 1])
        meta = sb("meta", [P, 3], BF16)
        meta_rest = sb("meta_rest", [P, 1])
        past_first = sb("past_first", [P, CAP])
        in_tile = sb("in_tile", [P, CAP], BF16)
        rank_e = sb("rank_e", [P, NE, P], BF16)
        meta_e = sb("meta_e", [P, NE, 3], BF16)
        slot_meta = sb("slot_meta", [P, SLOT_TILES, NE, 3])
        slot_first = sb("slot_first", [P, SLOT_TILES, NE])
        slot_local = sb("slot_local", [P, SLOT_TILES, NE])
        before = sb("before", [P, SLOT_TILES, P], BF16)
        tok_local = sb("tok_local", [P, NE, SLOT_TILES])
        tok_index = sb("tok_index", [P, NE, SLOT_TILES], I32)

        q_aug = sb("q_aug", [P, 2, 8, S], BF16)
        k_aug = sb("k_aug", [P, 2, 8, S], BF16)
        v_aug = sb("v_aug", [P, 2, 2, HEADS, 32])
        row_m = sb("row_m", [P, 2, HEADS])
        m_rest = sb("m_rest", [P, 2, HEADS])
        m_parts = sb("m_parts", [P, 2, 2, PARTS, 8], BF16)
        mT = sb("mT", [48, S], BF16)
        probs = sb("probs", [P, 6, 512])
        oT = sb("oT", [P, 2, 4, S])
        o_inv = sb("o_inv", [P, HEADS])
        o_nat = sb("o_nat", [P, HEADS, D])
        o_normT = sb("o_normT", [P, P])
        attn = sb("attn", [P, TILES, E])

        idx = sb("idx", [P, 2, SLOT_TILES], U32)
        w1_sb = sb("w1_sb", [P, 2, HID])
        w3_sb = sb("w3_sb", [P, 2, HID])
        w2_sb = sb("w2_sb", [P, 2, HC, E])
        xg = sb("xg", [P, 2, SLOT_TILES, ROW])
        xg_scaled = sb("xg_scaled", [P, SLOT_TILES, E])
        xgT = sb("xgT", [P, CAP])
        tanh_g = sb("tanh_g", [P, CAP])
        silu2 = sb("silu2", [P, CAP])
        hid = sb("hid", [P, HC, CAP])
        y_sb = sb("y_sb", [P, 2, SLOT_TILES, E])
        sums = sb("sums", [P, TILES, E])
        result = sb("result", [P, TILES, E])

        x_in = [sem(f"x_in{c}") for c in range(CHUNKS)]
        w_in = sem("w_in")
        wp_in = sem("wp_in")
        pool_ready = sem("pool_ready")
        consts_up = sem("consts_up")
        const_ps = sem("const_ps")
        const_sb = sem("const_sb")
        aug_ready = sem("aug_ready")
        stats_up = sem("stats_up")
        mv_up = sem("mv_up")
        var_up = sem("var_up")
        rstd_up = sem("rstd_up")
        xn_up = sem("xn_up")
        xT_ps = sem("xT_ps")
        xT_up = sem("xT_up")
        qk_ps = sem("qk_ps")
        vg_ps = sem("vg_ps")
        q_f_up = sem("q_f_up")
        k_f_up = sem("k_f_up")
        part0_up = sem("part0_up")
        rest_up = sem("rest_up")
        part1_up = sem("part1_up")
        part2_up = sem("part2_up")
        vg_up = sem("vg_up")
        parts_out = [sem("parts_out0"), sem("parts_out1")]
        x_bias_up = sem("x_bias_up")
        acc_out = sem("acc_out")
        gate_step = sem("gate_step")
        bits_up = sem("bits_up")
        gate_exp = sem("gate_exp")
        scores_up = sem("scores_up")
        table_out = sem("table_out")
        scT_ps = sem("scT_ps")
        search = sem("search")
        counted = sem("counted")
        count_ps = sem("count_ps")
        rejected = sem("rejected")
        next_up = sem("next_up")
        pick = sem("pick")
        gt_eq_up = sem("gt_eq_up")
        taken_up = sem("taken_up")
        rank_e_up = sem("rank_e_up")
        before_up = sem("before_up")
        tok_counted = sem("tok_counted")
        pick_ps = sem("pick_ps")
        slots_ps = sem("slots_ps")
        tok_up = sem("tok_up")

        qk_in = [[sem(f"qk_in{b}{hp}") for hp in range(2)] for b in range(2)]
        v_up = sem("v_up")
        nat_full = sem("nat_full")
        nat_max = sem("nat_max")
        m_step = sem("m_step")
        m_in = sem("m_in")
        tr_full = sem("tr_full")
        exp_up = sem("exp_up")
        probs_up = sem("probs_up")
        pv_quads = sem("pv_quads")
        oT_up = sem("oT_up")
        misc_full = sem("misc_full")
        misc_free = sem("misc_free")
        post_step = sem("post_step")
        idx_up = sem("idx_up")
        gathered = [sem("gathered0"), sem("gathered1")]
        ew_in = [sem("ew_in0"), sem("ew_in1")]
        scaled_up = sem("scaled_up")
        ff_full = sem("ff_full")
        tanh_up = sem("tanh_up")
        silu_up = sem("silu_up")
        hid_up = sem("hid_up")
        scattered = sem("scattered")
        sums_in = [sem(f"sums_in{c}") for c in range(CHUNKS)]
        result_up = sem("result_up")
        stored = sem("stored")

        USES = {
            "first": ("m0", "xgT", "mT", "y"),
            "mid": ("xgT", "o0", "mT", "a0", "pr0", "o1", "a1", "y", "pr1"),
            "last": ("xgT", "o0", "a0", "pr0", "o1", "a1", "y", "pr1"),
            "end": ("o0", "a0", "pr0", "o1", "a1", "pr1"),
        }

        def misc_base(n):
            return len(USES["first"]) + len(USES["mid"]) * (n - 1)

        def use(n, kind, name):
            at = USES[kind].index(name)
            if kind == "first":
                return at
            if kind == "end":
                return misc_base(B - 1) + len(USES["last"]) + at
            return misc_base(n) + at

        block = ctx.enter_context(nc.Block())

        @block.sync
        def _(sp):
            def load_experts(e, par):
                sp.dma_start(w1_sb[:, par, :], w1[e]).then_inc(ew_in[par], 16)
                sp.dma_start(w3_sb[:, par, :], w3[e]).then_inc(ew_in[par], 16)
                sp.dma_start(w2_sb[:, par], w2[e].rearrange("(c p) n -> p c n", p=P)).then_inc(ew_in[par], 16)

            def load_qk(n, par, hp):
                tok = bass.ds(n * S, S)
                row = 64 * hp
                for part, copies in ((0, 3), (1, 2), (2, 1)):
                    q = qk_dram[0, part, hp].rearrange("(d j) t -> d j t", j=8)[:, :, tok]
                    sp.dma_start(q_aug[row:row + copies * D, par],
                                 q.unsqueeze(0).broadcast_to([copies, D, 8, S])).then_inc(qk_in[par][hp], 16)
                    k = qk_dram[1, 0:copies, hp].rearrange("g (d j) t -> g d j t", j=8)[:, :, :, tok]
                    sp.dma_start(k_aug[row:row + copies * D, par], k).then_inc(qk_in[par][hp], 16)
                    row += copies * D

            def load_m(par, uses):
                sp.wait_ge(misc_free, uses + 1)
                for hp in range(2):
                    sp.dma_start(q_aug[64 * hp + KS:64 * hp + KM, par],
                                 mT[24 * hp:24 * hp + 24, :]).then_inc(m_in, 16)

            for c in range(CHUNKS):
                sp.dma_start(x_nat[:, CT * c:CT * c + CT], x_tok[:, CT * c:CT * c + CT]).then_inc(x_in[c], 16)
                if c == 0:
                    sp.dma_start(wqk_sb[:], w_qk).then_inc(w_in, 16)
                    sp.dma_start(bqk_sb[:], b_qk).then_inc(w_in, 16)
                    sp.dma_start(wvg_sb[:, 0:E], w_v).then_inc(w_in, 16)
                    sp.dma_start(wvg_sb[:, E:ROW], w_gate).then_inc(w_in, 16)
                    sp.dma_start(bv_sb[:], b_v.partition_broadcast(P)).then_inc(w_in, 16)
            sp.dma_start(bp_sb[:], b_p.partition_broadcast(P)).then_inc(wp_in, 16)
            sp.dma_start(wp_sb[:], w_p).then_inc(wp_in, 16)
            load_experts(0, 0)
            for c in range(CHUNKS):
                sp.wait_ge(part2_up, c + 1)
                for t in range(2):
                    sp.dma_start(qk_dram[t].rearrange("g hp r t -> (hp r) g t")[:, :, c * CHUNK:(c + 1) * CHUNK],
                                 qk_parts[:, c % 2, t]).then_inc(parts_out[c % 2], 16)
            sp.wait_ge(aug_ready, 1)
            sp.wait_ge(parts_out[0], 32 * (CHUNKS // 2))
            sp.wait_ge(parts_out[1], 32 * (CHUNKS // 2))
            for n in range(2):
                for hp in range(2):
                    load_qk(n, n, hp)
            sp.wait_ge(scores_up, 1)
            sp.dma_start(table.rearrange("(t p) r -> p t r", p=P), xn[:]).then_inc(table_out, 16)
            sp.wait_ge(x_bias_up, 1)
            sp.dma_start(acc.rearrange("(t p) e -> p t e", p=P), x_bias[:]).then_inc(acc_out, 16)
            load_m(0, use(0, "first", "m0"))

            def batch(n, par, is_first=False, load_next=True):
                if not is_first:
                    sp.wait_ge(misc_full, misc_base(n))
                load_experts(n + 1, 1 - par)
                if load_next:
                    sp.wait_ge(tr_full, 12 * n + 6)
                    load_qk(n + 2, par, 0)
                load_m(1 - par, use(n, "first" if is_first else "mid", "mT"))
                if load_next:
                    sp.wait_ge(tr_full, 12 * n + 12)
                    load_qk(n + 2, par, 1)

            batch(0, 0, is_first=True)
            with sp.Fori(0, (B - 2) // 2 - 1) as i:
                batch(2 * i + 1, 1)
                batch(2 * i + 2, 0)
            batch(B - 3, 1)
            batch(B - 2, 0, load_next=False)
            sp.wait_ge(scattered, 16 * SLOT_TILES * NE)
            sp.wait_ge(acc_out, 16)
            for c in range(CHUNKS):
                sp.dma_start(sums[:, CT * c:CT * c + CT],
                             acc.rearrange("(t p) e -> p t e", p=P)[:, CT * c:CT * c + CT]).then_inc(sums_in[c], 16)
            for c in range(CHUNKS):
                sp.wait_ge(result_up, c + 1)
                sp.dma_start(out_tok[:, CT * c:CT * c + CT], result[:, CT * c:CT * c + CT]).then_inc(stored, 16)
            sp.wait_ge(stored, 16 * CHUNKS)

        @block.gpsimd
        def _(pool):
            pool.memset(ones[:], 1.0).then_inc(consts_up, 1)
            pool.memset(ones16[:], 1.0).then_inc(consts_up, 1)
            pool.memset(zero16[:], 0.0).then_inc(consts_up, 1)
            pool.memset(neg_half[:], -0.5).then_inc(consts_up, 1)
            pool.wait_ge(consts_up, 4)
            pool.affine_select(out=ident[:], in_=ones[:], compare_op=ALU.is_equal, fill=0.0, base=0,
                               pattern=[[1, P]], channel_multiplier=-1).then_inc(consts_up, 1)
            pool.affine_select(out=ident16[:], in_=ones[:], compare_op=ALU.is_equal, fill=0.0, base=0,
                               pattern=[[1, P]], channel_multiplier=-1).then_inc(consts_up, 1)
            pool.affine_select(out=exp_of_row[:].rearrange("e (t f) -> e t f", f=NE),
                               in_=ones[0:NE].rearrange("e (t f) -> e t f", f=NE),
                               compare_op=ALU.is_equal, fill=0.0, base=0,
                               pattern=[[0, TILES], [1, NE]], channel_multiplier=-1).then_inc(consts_up, 1)
            for c in range(CHUNKS):
                pool.wait_ge(mv_up, CT * (c + 1))
                pool.tensor_scalar(var_eps[:, CT * c:CT * c + CT], mean_var[:, CT * c:CT * c + CT, 1],
                                   1e-5, None, ALU.add).then_inc(var_up, 1)
                pool.wait_ge(var_up, c + 1)
                pool.tensor_tensor(rstd[:, CT * c:CT * c + CT], var_eps[:, CT * c:CT * c + CT],
                                   neg_half[:], ALU.pow).then_inc(rstd_up, 1)
                if c == 1:
                    pool.affine_select(out=causal16[:], in_=zero16[:], compare_op=ALU.is_ge, fill=MASKED, base=0,
                                       pattern=[[0, 4], [-1, P]], channel_multiplier=1).then_inc(consts_up, 1)
            pool.memset(k_aug[:], -1.0).then_inc(aug_ready, 1)
            pool.memset(v_aug[:], 0.0).then_inc(aug_ready, 1)
            pool.wait_ge(aug_ready, 2)
            pool.memset(v_aug[:, :, :, :, D:D + 1], 1.0).then_inc(aug_ready, 1)
            pool.iota(slot_row[:], pattern=[[1, CAP]], base=0, channel_multiplier=0,
                      allow_small_or_imprecise_dtypes=True).then_inc(consts_up, 1)
            pool.iota(slot_col[:], pattern=[[P, SLOT_TILES]], base=0, channel_multiplier=1,
                      allow_small_or_imprecise_dtypes=True).then_inc(consts_up, 1)
            pool.iota(exponents[:], pattern=[[-1, TOP_BIT + 1]], base=127 + TOP_BIT,
                      channel_multiplier=0).then_inc(consts_up, 1)
            pool.wait_ge(const_sb, 2)
            pool.affine_select(out=prior16[:], in_=same16[:], compare_op=ALU.is_gt, fill=0.0, base=0,
                               pattern=[[1, P]], channel_multiplier=-1).then_inc(pool_ready, 1)
            pool.wait_ge(wp_in, 32)
            for c in range(CHUNKS):
                pool.wait_ge(x_in[c], 16)
            pool.tensor_tensor(x_bias[:], x_nat[:], bp_sb[:].unsqueeze(1).broadcast_to([P, TILES, E]),
                               ALU.add).then_inc(x_bias_up, 1)

            def settle():
                pool.nop(nofuse=True)

            def copy_v(n, par):
                for u in range(2):
                    pool.tensor_copy(v_aug[:, par, u, :, 0:D],
                                     v_nat[:, bass.ds(2 * n + u, 1), :].rearrange("p o (h d) -> p (o h) d", d=D)
                                     ).then_inc(v_up, 1)

            def gather(e, par):
                pool.tensor_copy(idx[:, par, :], tok_index[:, bass.ds(e, 1), :].rearrange("p o s -> p (o s)")
                                 ).then_inc(idx_up, 1)
                pool.wait_ge(idx_up, e + 1)
                settle()
                for s in range(SLOT_TILES):
                    pool.indirect_dma_start(
                        out=xg[:, par, s, :], out_offset=None, in_=table[:, :],
                        in_offset=bass.IndirectOffsetOnAxis(ap=idx[:, par, s:s + 1], axis=0)
                    ).then_inc(gathered[par], 16)

            def scatter(e, par, uses):
                pool.wait_ge(misc_free, uses)
                if not (isinstance(e, int) and e == 0):
                    pool.wait_ge(scattered, 16 * SLOT_TILES * e)
                settle()
                for s in range(SLOT_TILES):
                    pool.indirect_dma_start(
                        out=acc[:, :], out_offset=bass.IndirectOffsetOnAxis(ap=idx[:, par, s:s + 1], axis=0),
                        in_=y_sb[:, par, s, :], in_offset=None, compute_op=ALU.add
                    ).then_inc(scattered, 16)

            pool.wait_ge(vg_up, TILES)
            pool.wait_ge(aug_ready, 3)
            copy_v(0, 0)
            pool.wait_ge(table_out, 16)
            pool.wait_ge(acc_out, 16)
            pool.wait_ge(tok_up, 1)
            gather(0, 0)

            def mask_unit(n, q, j):
                pool.wait_ge(exp_up, 12 * n + 3 * q + j + 1)
                settle()
                v = probs[:, (3 * q + j) % 6, :]
                if j < 2:
                    v, heads = v.rearrange("p (h k) -> p h k", h=2)[:, :, 0:P], 2
                else:
                    v, heads = v.rearrange("p (h k) -> p h k", h=4), 4
                pool.affine_select(out=v, in_=v, compare_op=ALU.is_ge, fill=0.0, base=0,
                                   pattern=[[0, heads], [1, P]], channel_multiplier=-1).then_inc(probs_up, 1)

            def batch(n, par, kind):
                for q in range(4):
                    for j in range(3):
                        mask_unit(n, q, j)
                    if q == 0 and kind != "first":
                        scatter(n - 1, 1 - par, misc_base(n))
                    if q == 2 and kind != "last":
                        if kind != "first":
                            pool.wait_ge(scattered, 16 * SLOT_TILES * n)
                            pool.wait_ge(pv_quads, 4 * n)
                        copy_v(n + 1, 1 - par)
                        gather(n + 1, 1 - par)

            batch(0, 0, "first")
            with pool.Fori(0, (B - 2) // 2) as i:
                batch(2 * i + 1, 1, "mid")
                batch(2 * i + 2, 0, "mid")
            batch(B - 1, 1, "last")
            scatter(NE - 1, 1, use(B - 1, "last", "y") + 1)

        @block.scalar
        def _(act):
            for c in range(CHUNKS):
                act.wait_ge(xT_ps, c + 1)
                act.activation(xnT[:, c * CHUNK:(c + 1) * CHUNK], nat_ps[c % 2][:], ACT.Copy).then_inc(xT_up, 1)
                act.wait_ge(qk_ps, 2 * c + 2)
                if c == 0:
                    act.wait_ge(w_in, 80)
                else:
                    act.wait_ge(part2_up, c)
                act.activation(qk_f[:, 1], tr_ps[1][:], ACT.Identity, bias=bqk_sb[:, 1:2]).then_inc(k_f_up, 1)
                act.wait_ge(k_f_up, c + 1)
                act.wait_ge(q_f_up, c + 1)
                if c >= 2:
                    act.wait_ge(parts_out[c % 2], 32 * (c // 2))
                act.activation(qk_parts[:, c % 2, :, 0], qk_f[:], ACT.Copy).then_inc(part0_up, 1)
                act.wait_ge(rest_up, c + 1)
                act.activation(qk_parts[:, c % 2, :, 1], qk_rest[:], ACT.Copy).then_inc(part1_up, 1)
            act.wait_ge(gate_step, 2)
            act.activation(exped[:], shifted[:], ACT.Exp).then_inc(gate_exp, 1)

            def exp_unit(n, q, j, kind):
                act.wait_ge(tr_full, 12 * n + 3 * q + j + 1)
                if j == 0 and not (kind == "first" and q < 2):
                    act.wait_ge(pv_quads, 4 * n + q - 1)
                act.activation(probs[:, (3 * q + j) % 6, :], tr_ps[(3 * q + j) % 2][:], ACT.Exp).then_inc(exp_up, 1)

            def take_o(n, half, par):
                act.wait_ge(pv_quads, 4 * n + 2 * half + 2)
                act.activation(oT[:, par, 2 * half:2 * half + 2, :], pv_ps[:].rearrange("p (q t) -> p q t", q=2),
                               ACT.Copy).then_inc(oT_up, 1)

            def tanh(e, c, kind):
                act.wait_ge(ff_full, 4 * e + 2 * c + 1)
                if not (kind == "first" and c == 0):
                    act.wait_ge(silu_up, 2 * e + c)
                act.activation(tanh_g[:], ff_ps[0][:], ACT.Tanh, scale=0.5).then_inc(tanh_up, 1)

            def batch(n, par, kind):
                for q in range(4):
                    for j in range(3):
                        exp_unit(n, q, j, kind)
                    if q == 0 and kind != "first":
                        take_o(n - 1, 1, 1 - par)
                    if q == 1:
                        tanh(n, 0, kind)
                    if q == 2:
                        if kind != "first":
                            act.wait_ge(misc_full, misc_base(n))
                        take_o(n, 0, par)
                        tanh(n, 1, kind)

            batch(0, 0, "first")
            with act.Fori(0, (B - 2) // 2) as i:
                batch(2 * i + 1, 1, "mid")
                batch(2 * i + 2, 0, "mid")
            batch(B - 1, 1, "last")
            take_o(B - 1, 1, 1)

        @block.vector
        def _(dve):
            def normalize(c):
                dve.wait_ge(x_in[c], 16)
                tiles = range(CT * c, CT * c + CT)
                for t in tiles:
                    dve.bn_stats(stats[:, t, :], x_nat[:, t, :]).then_inc(stats_up, 1)
                for t in tiles:
                    dve.wait_ge(stats_up, t + 1)
                    dve.bn_aggr(mean_var[:, t, :], stats[:, t, :]).then_inc(mv_up, 1)
                dve.wait_ge(rstd_up, c + 1)
                for t in tiles:
                    dve.tensor_scalar(xn[:, t, 0:E], x_nat[:, t, :], mean_var[:, t, 0:1], rstd[:, t:t + 1],
                                      ALU.subtract, ALU.mult).then_inc(xn_up, 1)

            def split(c):
                if c == 0:
                    dve.wait_ge(w_in, 80)
                dve.wait_ge(qk_ps, 2 * c + 1)
                dve.tensor_scalar(qk_f[:, 0], tr_ps[0][:], bqk_sb[:, 0:1], INV_SQRT_D,
                                  ALU.add, ALU.mult).then_inc(q_f_up, 1)
                dve.wait_ge(part0_up, c + 1)
                part = qk_parts[:, c % 2]
                dve.tensor_tensor(qk_rest[:], qk_f[:], part[:, :, 0], ALU.subtract).then_inc(rest_up, 1)
                dve.wait_ge(part1_up, c + 1)
                dve.tensor_tensor(part[:, :, 2], qk_rest[:], part[:, :, 1], ALU.subtract).then_inc(part2_up, 1)
                for u in range(2):
                    dve.wait_ge(vg_ps, 2 * c + u + 1)
                    t = CT * c + 2 * u
                    ps = ff_ps[u][:, 0:2 * ROW].rearrange("p (t r) -> p t r", t=2)
                    dve.tensor_tensor(v_nat[:, t:t + 2, :], ps[:, :, 0:E],
                                      bv_sb[:].unsqueeze(1).broadcast_to([P, 2, E]), ALU.add).then_inc(vg_up, 1)
                    dve.tensor_copy(logits[:, t:t + 2, :], ps[:, :, E:ROW]).then_inc(vg_up, 1)

            normalize(0)
            dve.wait_ge(const_ps, 1)
            dve.tensor_copy(same16[:], misc_ps[:, 0:P]).then_inc(const_sb, 1)
            dve.tensor_copy(sel_exp[:], misc_ps[:, P:P + NE]).then_inc(const_sb, 1)
            for c in range(CHUNKS):
                if c + 1 < CHUNKS:
                    normalize(c + 1)
                split(c)
            dve.wait_ge(consts_up, 11)
            dve.tensor_scalar(bits_f[:].bitcast(I32), exponents[:], 23, None,
                              ALU.logical_shift_left).then_inc(bits_up, 1)
            dve.memset(cand[:], CAND_START).then_inc(bits_up, 1)
            dve.wait_ge(bits_up, 2)
            dve.tensor_copy(bits_i[:], bits_f[:]).then_inc(bits_up, 1)

            def spread(a):
                return a[:].unsqueeze(2).broadcast_to([P, TILES, NE])

            dve.wait_ge(vg_up, TILES)
            dve.tensor_reduce(row_max[:], logits[:], AX_X, ALU.max).then_inc(gate_step, 1)
            dve.wait_ge(gate_step, 1)
            dve.tensor_tensor(shifted[:], logits[:], spread(row_max), ALU.subtract).then_inc(gate_step, 1)
            dve.wait_ge(gate_exp, 1)
            dve.tensor_reduce(row_sum[:], exped[:], AX_X, ALU.add).then_inc(gate_step, 1)
            dve.wait_ge(gate_step, 3)
            dve.reciprocal(row_inv[:], row_sum[:]).then_inc(gate_step, 1)
            dve.wait_ge(gate_step, 4)
            dve.tensor_tensor(scores[:], exped[:], spread(row_inv), ALU.mult).then_inc(gate_step, 1)
            dve.wait_ge(gate_step, 5)
            dve.tensor_copy(xn[:, :, E:ROW], scores[:]).then_inc(scores_up, 1)
            dve.wait_ge(scT_ps, 1)
            dve.tensor_copy(scoresT[:], misc_ps[:, 0:P]).then_inc(search, 1)

            dve.wait_ge(search, 1)
            dve.wait_ge(bits_up, 3)

            def try_bit():
                dve.tensor_scalar(cmp[:], scoresT[:], cand[:].bitcast(F32), 0.0, ALU.is_ge, ALU.add,
                                  accum_out=count[:]).then_inc(counted, 1)

            LOOPS = TOP_BIT
            with dve.Fori(0, LOOPS) as i:
                dve.wait_ge(search, i + 1)
                try_bit()
                dve.tensor_tensor(cand_next[:], cand[:], bits_i[:, bass.ds(i + 1, 1)],
                                  ALU.bitwise_or).then_inc(next_up, 1)
                dve.wait_ge(count_ps, i + 1)
                dve.scalar_tensor_tensor(out=reject[:], in0=misc_ps[:, 0:1], scalar=CAP - 0.5,
                                         in1=bits_f[:, bass.ds(i, 1)], op0=ALU.is_lt, op1=ALU.mult
                                         ).then_inc(rejected, 1)
                dve.wait_ge(rejected, i + 1)
                dve.wait_ge(next_up, i + 1)
                dve.tensor_tensor(cand[:], cand_next[:], reject[:], ALU.bitwise_xor).then_inc(search, 1)
            dve.wait_ge(search, LOOPS + 1)
            try_bit()
            dve.wait_ge(count_ps, LOOPS + 1)
            dve.tensor_scalar(reject[:], misc_ps[:, 0:1], CAP - 0.5, None, ALU.is_lt).then_inc(rejected, 1)
            dve.wait_ge(rejected, LOOPS + 1)
            dve.tensor_tensor(cand[:], cand[:], reject[:], ALU.bitwise_xor).then_inc(search, 1)
            dve.wait_ge(search, LOOPS + 2)

            steps = [0]

            def link(ins):
                steps[0] += 1
                ins.then_inc(pick, 1)
                dve.wait_ge(pick, steps[0])

            limit = cand[:].bitcast(F32)
            link(dve.tensor_scalar(above[:], scoresT[:], limit, 0.0, ALU.is_gt, ALU.add, accum_out=gt_eq[:, 0:1]))
            link(dve.tensor_scalar(equal[:], scoresT[:], limit, 0.0, ALU.is_equal, ALU.add, accum_out=gt_eq[:, 1:2]))
            dve.tensor_copy(gt_eq16[:], gt_eq[:]).then_inc(gt_eq_up, 1)
            dve.wait_ge(pick_ps, 1)
            link(dve.tensor_scalar(need[:], misc_ps[:, 0:1], -1.0, float(CAP), ALU.mult, ALU.add))
            link(dve.tensor_copy(eq_prior[:], misc_ps[:, 1:2]))
            link(dve.tensor_tensor_scan(eq_rank[:], ones[:], equal[:], eq_prior[:], ALU.mult, ALU.add))
            link(dve.scalar_tensor_tensor(out=eq_kept[:], in0=eq_rank[:], scalar=need[:], in1=equal[:],
                                          op0=ALU.is_le, op1=ALU.mult))
            link(dve.tensor_tensor(chosen[:], above[:], eq_kept[:], ALU.add))
            link(dve.tensor_tensor_scan(rank[:], ones[:], chosen[:], 0.0, ALU.mult, ALU.add))
            dve.tensor_copy(taken16[:], rank[:, P - 1:P]).then_inc(taken_up, 1)
            dve.wait_ge(pick_ps, 2)
            link(dve.tensor_copy(first[:], misc_ps[:, 0:1]))
            link(dve.tensor_copy(meta[:, 0:1], misc_ps[:, 1:2]))
            link(dve.tensor_tensor(last[:], first[:], rank[:, P - 1:P], ALU.add))
            link(dve.tensor_copy(meta[:, 1:2], first[:]))
            link(dve.tensor_tensor(meta[:, 2:3], first[:], meta[:, 1:2], ALU.subtract))
            link(dve.tensor_scalar(past_first[:], slot_row[:], first[:], None, ALU.is_ge))
            link(dve.scalar_tensor_tensor(out=in_tile[:], in0=slot_row[:], scalar=last[:], in1=past_first[:],
                                          op0=ALU.is_lt, op1=ALU.mult))
            link(dve.tensor_tensor(meta_e[:], meta[:].unsqueeze(1).broadcast_to([P, NE, 3]),
                                   sel_exp[:].unsqueeze(2).broadcast_to([P, NE, 3]), ALU.mult))
            dve.tensor_tensor(rank_e[:], rank[:].unsqueeze(1).broadcast_to([P, NE, P]),
                              sel_exp[:].unsqueeze(2).broadcast_to([P, NE, P]), ALU.mult).then_inc(rank_e_up, 1)
            dve.wait_ge(slots_ps, 1)
            link(dve.tensor_copy(slot_meta[:], tr_ps[0][:, 0:SLOT_TILES * NE * 3].rearrange(
                "p (s e m) -> p s e m", s=SLOT_TILES, e=NE)))
            link(dve.tensor_tensor(slot_first[:], slot_meta[:, :, :, 1], slot_meta[:, :, :, 2], ALU.add))
            link(dve.tensor_tensor(slot_local[:], slot_col[:].unsqueeze(2).broadcast_to([P, SLOT_TILES, NE]),
                                   slot_first[:], ALU.subtract))
            for e in range(NE):
                dve.wait_ge(slots_ps, e + 2)
                if e > 0:
                    dve.wait_ge(tok_counted, e)
                dve.tensor_tensor(before[:], nat_ps[e % 2][:].rearrange("p (s t) -> p s t", s=SLOT_TILES),
                                  slot_local[:, :, e:e + 1].broadcast_to([P, SLOT_TILES, P]),
                                  ALU.is_le).then_inc(before_up, 1)
                dve.wait_ge(before_up, e + 1)
                dve.tensor_reduce(tok_local[:, e, :], before[:], AX_X, ALU.add).then_inc(tok_counted, 1)
            dve.wait_ge(tok_counted, NE)
            dve.scalar_tensor_tensor(out=tok_index[:], in0=slot_meta[:, :, :, 0].rearrange("p s e -> p e s"),
                                     scalar=float(P), in1=tok_local[:], op0=ALU.mult, op1=ALU.add
                                     ).then_inc(tok_up, 1)

            def max_unit(n, q, j):
                dve.wait_ge(nat_full, 12 * n + 3 * q + j + 1)
                if j == 0:
                    dst, heads = row_m[:, 0, 4 * q:4 * q + 4], 4
                else:
                    h = 4 * q + 2 * (j - 1)
                    dst, heads = row_m[:, 1, h:h + 2], 2
                dve.tensor_reduce(dst, nat_ps[(3 * q + j) % 2][:].rearrange("p (h k) -> p h k", h=heads),
                                  AX_X, ALU.max).then_inc(nat_max, 1)

            def split_m(n):
                m = row_m[:].rearrange("p u (g j) -> p u g j", g=2)
                rest = m_rest[:].rearrange("p u (g j) -> p u g j", g=2)
                dve.wait_ge(nat_max, 12 * n + 12)
                dve.tensor_copy(m_parts[:, :, :, 0, :], m).then_inc(m_step, 1)
                dve.wait_ge(m_step, 4 * n + 1)
                dve.tensor_tensor(rest, m, m_parts[:, :, :, 0, :], ALU.subtract).then_inc(m_step, 1)
                dve.wait_ge(m_step, 4 * n + 2)
                dve.tensor_copy(m_parts[:, :, :, 1, :], rest).then_inc(m_step, 1)
                dve.wait_ge(m_step, 4 * n + 3)
                dve.tensor_tensor(m_parts[:, :, :, 2, :], rest, m_parts[:, :, :, 1, :],
                                  ALU.subtract).then_inc(m_step, 1)

            def take_mT(n, uses):
                dve.wait_ge(misc_full, uses + 1)
                if not (isinstance(n, int) and n == 0):
                    dve.wait_ge(m_in, 32 * n)
                dve.tensor_copy(mT[:], misc_ps[:].bitcast(BF16)[0:48, 0:S]).then_inc(misc_free, 1)

            for q in range(4):
                for j in range(3):
                    max_unit(0, q, j)
            split_m(0)
            take_mT(0, use(0, "first", "m0"))

            def scale_rows(e, par):
                dve.wait_ge(gathered[par], 8 * SLOT_TILES * (e - par) + 16 * SLOT_TILES)
                dve.tensor_tensor(xg_scaled[:], xg[:, par, :, 0:E],
                                  xg[:, par, :, bass.ds(E + e, 1)].broadcast_to([P, SLOT_TILES, E]),
                                  ALU.mult).then_inc(scaled_up, 1)

            def take_xT(uses):
                dve.wait_ge(misc_full, uses + 1)
                dve.tensor_copy(xgT[:], misc_ps[:]).then_inc(misc_free, 1)

            def take_o(k, uses):
                o = misc_ps[:].rearrange("p (h r) -> p h r", r=32)
                dve.wait_ge(misc_full, uses + 1)
                dve.reciprocal(o_inv[:], o[:, :, D]).then_inc(post_step, 1)
                dve.wait_ge(post_step, k + 1)
                dve.tensor_tensor(o_nat[:], o[:, :, 0:D], o_inv[:].unsqueeze(2).broadcast_to([P, HEADS, D]),
                                  ALU.mult).then_inc(misc_free, 1)

            def take_a(uses):
                dve.wait_ge(misc_full, uses + 1)
                dve.tensor_copy(o_normT[:], misc_ps[:, 0:P]).then_inc(misc_free, 1)

            def take_pr(n, u, uses):
                dve.wait_ge(misc_full, uses + 1)
                dve.tensor_copy(attn[:, bass.ds(2 * n + u, 1), :], misc_ps[:, 0:E].unsqueeze(1)
                                ).then_inc(misc_free, 1)

            def gated(e, c):
                dve.wait_ge(tanh_up, 2 * e + c + 1)
                dve.scalar_tensor_tensor(out=silu2[:], in0=tanh_g[:], scalar=1.0, in1=ff_ps[0][:],
                                         op0=ALU.add, op1=ALU.mult).then_inc(silu_up, 1)
                dve.wait_ge(silu_up, 2 * e + c + 1)
                dve.wait_ge(ff_full, 4 * e + 2 * c + 2)
                dve.scalar_tensor_tensor(out=hid[:, c, :], in0=silu2[:], scalar=0.5, in1=ff_ps[1][:],
                                         op0=ALU.mult, op1=ALU.mult).then_inc(hid_up, 1)

            def take_y(e, par, uses, kind):
                dve.wait_ge(misc_full, uses + 1)
                if kind != "first":
                    if not (isinstance(e, int) and e < 2):
                        dve.wait_ge(scattered, 16 * SLOT_TILES * (e - 1))
                dve.tensor_copy(y_sb[:, par], misc_ps[:].rearrange("p (s n) -> p s n", s=SLOT_TILES)
                                ).then_inc(misc_free, 1)

            def batch(n, par, kind):
                def at(name):
                    return use(n, kind, name)

                scale_rows(n, par)
                for q in range(4):
                    if q < 2 and kind != "last":
                        for r in range(2 * q, 2 * q + 2):
                            for j in range(3):
                                max_unit(n + 1, r, j)
                    if q == 0:
                        take_xT(at("xgT"))
                    if q == 1 and kind != "first":
                        take_o(2 * (n - 1), at("o0"))
                    if q == 2:
                        if kind != "last":
                            split_m(n + 1)
                            take_mT(n + 1, at("mT"))
                        if kind != "first":
                            take_a(at("a0"))
                        gated(n, 0)
                    if q == 3:
                        if kind != "first":
                            take_pr(n - 1, 0, at("pr0"))
                            take_o(2 * (n - 1) + 1, at("o1"))
                        gated(n, 1)
                        if kind != "first":
                            take_a(at("a1"))
                        take_y(n, par, at("y"), kind)
                        if kind != "first":
                            take_pr(n - 1, 1, at("pr1"))

            batch(0, 0, "first")
            with dve.Fori(0, (B - 2) // 2) as i:
                batch(2 * i + 1, 1, "mid")
                batch(2 * i + 2, 0, "mid")
            batch(B - 1, 1, "last")
            for u in range(2):
                take_o(2 * (B - 1) + u, use(B - 1, "end", f"o{u}"))
                take_a(use(B - 1, "end", f"a{u}"))
                take_pr(B - 1, u, use(B - 1, "end", f"pr{u}"))
            dve.wait_ge(misc_free, use(B - 1, "end", "pr1") + 1)
            for c in range(CHUNKS):
                dve.wait_ge(sums_in[c], 16)
                dve.tensor_tensor(result[:, CT * c:CT * c + CT], attn[:, CT * c:CT * c + CT],
                                  sums[:, CT * c:CT * c + CT], ALU.add).then_inc(result_up, 1)

        @block.tensor
        def _(pe):
            pe.wait_ge(consts_up, 7)
            pe.matmul(misc_ps[:, 0:P], exp_of_row[:], exp_of_row[:], start=True, stop=True)
            pe.matmul(misc_ps[:, P:P + NE], exp_of_row[:], ident16[0:NE, 0:NE], start=True,
                      stop=True).then_inc(const_ps, 1)

            for c in range(CHUNKS):
                pe.wait_ge(xn_up, CT * c + CT)
                if c >= 2:
                    pe.wait_ge(xT_up, c - 1)
                for u in range(CT):
                    ins = pe.transpose(nat_ps[c % 2][:, u * P:(u + 1) * P], xn[:, CT * c + u, 0:E], ident[:])
                ins.then_inc(xT_ps, 1)
                pe.wait_ge(xT_up, c + 1)
                if c == 0:
                    pe.wait_ge(w_in, 80)
                else:
                    pe.wait_ge(q_f_up, c)
                    pe.wait_ge(k_f_up, c)
                    pe.wait_ge(vg_up, CT * c)
                for t in range(2):
                    pe.matmul(tr_ps[t][:], wqk_sb[:, t, :], xnT[:, c * CHUNK:(c + 1) * CHUNK],
                              start=True, stop=True).then_inc(qk_ps, 1)
                for u in range(2):
                    for v in range(2):
                        t = CT * c + 2 * u + v
                        ins = pe.matmul(ff_ps[u][:, v * ROW:(v + 1) * ROW], xnT[:, t * P:(t + 1) * P], wvg_sb[:],
                                        start=True, stop=True)
                    ins.then_inc(vg_ps, 1)

            pe.wait_ge(const_sb, 2)
            pe.wait_ge(scores_up, 1)
            pe.transpose(misc_ps[:, 0:P], scores[:].rearrange("p t e -> p (t e)"), ident[:]).then_inc(scT_ps, 1)

            pe.wait_ge(search, 1)
            with pe.Fori(0, TOP_BIT + 1) as i:
                pe.wait_ge(counted, i + 1)
                pe.matmul(misc_ps[:, 0:1], same16[:], count[:], start=True, stop=True).then_inc(count_ps, 1)

            pe.wait_ge(gt_eq_up, 1)
            pe.wait_ge(pool_ready, 1)
            pe.matmul(misc_ps[:, 0:1], same16[:], gt_eq16[:, 0:1], start=True, stop=True)
            pe.matmul(misc_ps[:, 1:2], prior16[:], gt_eq16[:, 1:2], start=True, stop=True).then_inc(pick_ps, 1)
            pe.wait_ge(taken_up, 1)
            pe.matmul(misc_ps[:, 0:1], prior16[:], taken16[:], start=True, stop=True)
            pe.matmul(misc_ps[:, 1:2], prior16[:], ones16[:], start=True, stop=True).then_inc(pick_ps, 1)
            pe.wait_ge(rank_e_up, 1)
            for s in range(SLOT_TILES):
                ins = pe.matmul(tr_ps[0][:, s * NE * 3:(s + 1) * NE * 3], in_tile[:, s * P:(s + 1) * P],
                                meta_e[:].rearrange("p e m -> p (e m)"), start=True, stop=True)
            ins.then_inc(slots_ps, 1)
            for e in range(NE):
                if e >= 2:
                    pe.wait_ge(before_up, e - 1)
                for s in range(SLOT_TILES):
                    ins = pe.matmul(nat_ps[e % 2][:, s * P:(s + 1) * P], in_tile[:, s * P:(s + 1) * P],
                                    rank_e[:, e, :], start=True, stop=True)
                ins.then_inc(slots_ps, 1)

            def nat_unit(n, par, q, j):
                hp = q // 2
                lo = 64 * hp
                ps = nat_ps[(3 * q + j) % 2]
                if j == 0 and q in (0, 2):
                    pe.wait_ge(qk_in[par][hp], 48 * (n - par) + 96)
                if not (isinstance(n, int) and n == 0 and q == 0 and j < 2):
                    pe.wait_ge(nat_max, 12 * n + 3 * q + j - 1)
                if j == 0:
                    pe.matmul(ps[:], ident16[:], causal16[:].rearrange("p a k -> p (a k)"), start=True, stop=False,
                              skip_group_check=True)
                    for c in range(4):
                        jj = (4 * q + c) % 8
                        ins = pe.matmul(ps[:, c * P:(c + 1) * P], q_aug[lo:lo + KS, par, jj, 0:P],
                                        k_aug[lo:lo + KS, par, jj, 0:P], start=False, stop=True,
                                        skip_group_check=True)
                else:
                    pe.matmul(ps[:].rearrange("p (h k) -> p h k", h=2)[:, :, P:S], ident16[:], causal16[:, 0:2, :],
                              start=True, stop=False, skip_group_check=True)
                    for c in range(2):
                        jj = (4 * q + 2 * (j - 1) + c) % 8
                        ins = pe.matmul(ps[:, c * S:(c + 1) * S], q_aug[lo:lo + KS, par, jj, P:S],
                                        k_aug[lo:lo + KS, par, jj, 0:S], start=False, stop=True,
                                        skip_group_check=True)
                ins.then_inc(nat_full, 1)

            def tr_unit(n, par, q, j, kind):
                hp = q // 2
                lo = 64 * hp
                ps = tr_ps[(3 * q + j) % 2]
                if q == 0 and j == 0:
                    pe.wait_ge(m_in, 32 * (n + 1))
                if not (kind == "first" and q == 0 and j < 2):
                    pe.wait_ge(exp_up, 12 * n + 3 * q + j - 1)
                if j < 2:
                    for c in range(2):
                        jj = (4 * q + 2 * j + c) % 8
                        ins = pe.matmul(ps[:, c * S:(c + 1) * S], k_aug[lo:lo + KM, par, jj, 0:P],
                                        q_aug[lo:lo + KM, par, jj, :], start=True, stop=True)
                else:
                    for c in range(4):
                        jj = (4 * q + c) % 8
                        ins = pe.matmul(ps[:, c * P:(c + 1) * P], k_aug[lo:lo + KM, par, jj, P:S],
                                        q_aug[lo:lo + KM, par, jj, P:S], start=True, stop=True)
                ins.then_inc(tr_full, 1)

            def pv(n, par, q, kind):
                pe.wait_ge(probs_up, 12 * n + 3 * q + 3)
                if q == 0:
                    pe.wait_ge(v_up, 2 * n + 2)
                if q % 2 == 0 and not (kind == "first" and q == 0):
                    pe.wait_ge(oT_up, 2 * n + q // 2)
                col = (q % 2) * S
                for c in range(4):
                    pe.matmul(pv_ps[32 * c:32 * c + 32, col:col + S], v_aug[:, par, 0, 4 * q + c, :],
                              probs[:, (3 * q + c // 2) % 6, (c % 2) * S:(c % 2) * S + S], start=True, stop=False,
                              tile_position=(0, 32 * c), skip_group_check=True)
                for c in range(4):
                    ins = pe.matmul(pv_ps[32 * c:32 * c + 32, col + P:col + S], v_aug[:, par, 1, 4 * q + c, :],
                                    probs[:, (3 * q + 2) % 6, c * P:(c + 1) * P], start=False, stop=True,
                                    tile_position=(0, 32 * c), skip_group_check=True)
                ins.then_inc(pv_quads, 1)

            def misc_wait(uses):
                if not (isinstance(uses, int) and uses == 0):
                    pe.wait_ge(misc_free, uses)

            def turn_m(uses):
                misc_wait(uses)
                pe.nop(nofuse=True)
                for u in range(2):
                    ins = pe.transpose(misc_ps[:].bitcast(BF16)[0:48, u * P:(u + 1) * P],
                                       m_parts[:, u].rearrange("p g s j -> p (g s j)"), ident16[:])
                ins.then_inc(misc_full, 1)

            def turn_rows(e, uses):
                misc_wait(uses)
                pe.wait_ge(scaled_up, e + 1)
                for s in range(SLOT_TILES):
                    ins = pe.transpose(misc_ps[:, s * P:(s + 1) * P], xg_scaled[:, s, :], ident[:])
                ins.then_inc(misc_full, 1)

            def gate_up(e, par, c, uses):
                if c == 0:
                    pe.wait_ge(misc_free, uses + 1)
                    pe.wait_ge(ew_in[par], 24 * (e - par) + 48)
                if not (isinstance(e, int) and e == 0 and c == 0):
                    pe.wait_ge(hid_up, 2 * e + c)
                pe.matmul(ff_ps[0][:], w1_sb[:, par, c * P:(c + 1) * P], xgT[:], start=True, stop=True
                          ).then_inc(ff_full, 1)
                pe.matmul(ff_ps[1][:], w3_sb[:, par, c * P:(c + 1) * P], xgT[:], start=True, stop=True
                          ).then_inc(ff_full, 1)

            def down(e, par, uses):
                misc_wait(uses)
                pe.wait_ge(hid_up, 2 * e + 2)
                for s in range(SLOT_TILES):
                    for c in range(HC):
                        ins = pe.matmul(misc_ps[:, s * P:(s + 1) * P], hid[:, c, s * P:(s + 1) * P],
                                        w2_sb[:, par, c, :], start=(c == 0), stop=(c == HC - 1))
                ins.then_inc(misc_full, 1)

            def turn_o(n, par, u, uses):
                misc_wait(uses)
                pe.wait_ge(oT_up, 2 * n + 2)
                for q in range(4):
                    ins = pe.transpose(misc_ps[:, q * P:(q + 1) * P], oT[:, par, q, u * P:(u + 1) * P], ident[:])
                ins.then_inc(misc_full, 1)

            def turn_a(uses):
                misc_wait(uses)
                pe.transpose(misc_ps[:, 0:P], o_nat[:].rearrange("p h d -> p (h d)"), ident[:]).then_inc(misc_full, 1)

            def project(uses):
                misc_wait(uses)
                pe.matmul(misc_ps[:, 0:E], o_normT[:], wp_sb[:], start=True, stop=True).then_inc(misc_full, 1)

            for q in range(4):
                for j in range(3):
                    if q == 0 and j == 0:
                        pe.wait_ge(tok_up, 1)
                        pe.wait_ge(consts_up, 11)
                        pe.wait_ge(wp_in, 32)
                    nat_unit(0, 0, q, j)
            pe.wait_ge(m_step, 4)
            turn_m(0)

            def batch(n, par, kind):
                def at(name):
                    return use(n, kind, name)

                for q in range(4):
                    for j in range(3):
                        tr_unit(n, par, q, j, kind)
                        if q < 2 and kind != "last":
                            for k in (2 * j, 2 * j + 1):
                                nat_unit(n + 1, 1 - par, 2 * q + k // 3, k % 3)
                    if q > 0:
                        pv(n, par, q - 1, kind)
                    elif kind != "first":
                        pv(n - 1, 1 - par, 3, kind)
                    if q == 0:
                        turn_rows(n, at("xgT"))
                    if q == 1:
                        if kind != "first":
                            turn_o(n - 1, 1 - par, 0, at("o0"))
                        gate_up(n, par, 0, at("xgT"))
                    if q == 2:
                        if kind != "last":
                            pe.wait_ge(m_step, 4 * (n + 1) + 4)
                            turn_m(at("mT"))
                        if kind != "first":
                            turn_a(at("a0"))
                        gate_up(n, par, 1, None)
                    if q == 3:
                        if kind != "first":
                            project(at("pr0"))
                            turn_o(n - 1, 1 - par, 1, at("o1"))
                            turn_a(at("a1"))
                        down(n, par, at("y"))
                        if kind != "first":
                            project(at("pr1"))

            batch(0, 0, "first")
            with pe.Fori(0, (B - 2) // 2) as i:
                batch(2 * i + 1, 1, "mid")
                batch(2 * i + 2, 0, "mid")
            batch(B - 1, 1, "last")
            pv(B - 1, 1, 3, "last")
            for u in range(2):
                turn_o(B - 1, 1, u, use(B - 1, "end", f"o{u}"))
                turn_a(use(B - 1, "end", f"a{u}"))
                project(use(B - 1, "end", f"pr{u}"))


def kernel(**inputs):
    import numpy as np
    import concourse.bacc as bacc
    from concourse import mybir as _mybir
    from concourse.bass_utils import run_bass_kernel_spmd as run

    x = np.ascontiguousarray(inputs["L0_attn_x"])
    E = x.shape[-1]
    w = np.asarray(inputs["L0_attn_W1"]).reshape(E, 2, HEADS // 2, 3, E // HEADS)
    b = np.asarray(inputs["L0_attn_b1"]).reshape(2, HEADS // 2, 3, E // HEADS)
    arrays = {
        "x": x,
        "w_qk": w[:, :, :, 0:2].transpose(0, 3, 1, 4, 2).reshape(E, 2, E),
        "b_qk": b[:, :, 0:2].transpose(0, 3, 1, 2).reshape(E, 2),
        "w_v": w[:, :, :, 2].reshape(E, E),
        "b_v": b[:, :, 2].reshape(E),
        "w_p": np.asarray(inputs["L0_attn_Wp"]),
        "b_p": np.asarray(inputs["L0_attn_bp"]),
        "w_gate": np.asarray(inputs["L0_ffn_wg"]),
        "w1": np.asarray(inputs["L0_ffn_w1"]),
        "w3": np.asarray(inputs["L0_ffn_w3"]),
        "w2": np.asarray(inputs["L0_ffn_w2"]),
    }
    arrays = {k: np.ascontiguousarray(v) for k, v in arrays.items()}
    nc = bacc.Bacc("TRN2", target_bir_lowering=False, num_devices=1)
    args = [nc.dram_tensor(k, v.shape, _mybir.dt.from_np(v.dtype), kind="ExternalInput").ap()
            for k, v in arrays.items()]
    out = nc.dram_tensor("out", x.shape, _mybir.dt.from_np(x.dtype), kind="ExternalOutput").ap()
    attention_moe_block(nc, *args, out)
    r = run(nc, [arrays], core_ids=[0])
    return r.results[0]["out"]
```

```python
from contextlib import ExitStack

import concourse.bass as bass
from concourse import mybir

ALU = mybir.AluOpType
ACT = mybir.ActivationFunctionType
F32 = mybir.dt.float32
BF16 = mybir.dt.bfloat16
I32 = mybir.dt.int32
U32 = mybir.dt.uint32
AX_X = mybir.AxisListType.X

P = 128
HEADS = 16
TOP_BIT = 29
CAND_START = 1 << TOP_BIT


def attention_moe_block(nc, x, w_qk, b_qk, w_v, b_v, w_p, b_p, w_gate, w1, w3, w2, out):
    B, S, E = x.shape
    NE, _, HID = w1.shape
    TOKENS = B * S
    TILES = TOKENS // P
    CAP = TOKENS // 4
    SLOT_TILES = CAP // P
    HC = HID // P
    D = E // HEADS
    CHUNK = 512
    CT = CHUNK // P
    CHUNKS = TOKENS // CHUNK
    PARTS = 3
    KS = PARTS * PARTS * D
    KM = KS + PARTS
    ROW = E + NE
    INV_SQRT_D = float(D) ** -0.5
    MASKED = -1.0e6
    assert E == P and S == 2 * P and NE == B and HEADS == 16 and CAP == CHUNK and TILES * NE == P

    x_tok = x.rearrange("b (u p) e -> p (b u) e", p=P)
    out_tok = out.rearrange("b (u p) e -> p (b u) e", p=P)

    with ExitStack() as ctx:
        def sb(name, shape, dt=F32):
            return ctx.enter_context(nc.sbuf_tensor(name, shape, dt))

        def bank(name):
            return ctx.enter_context(nc.psum_tensor(name, [P, 512], F32))

        def sem(name):
            return ctx.enter_context(nc.semaphore(name))

        table = nc.dram_tensor("token_table", (TOKENS, ROW), F32).ap()
        acc = nc.dram_tensor("expert_sum", (TOKENS, E), F32).ap()
        qk_dram = nc.dram_tensor("qk_parts", (2, PARTS, 2, P // 2, TOKENS), BF16).ap()

        nat_ps = [bank("nat_ps0"), bank("nat_ps1")]
        tr_ps = [bank("tr_ps0"), bank("tr_ps1")]
        pv_ps = bank("pv_ps")
        ff_ps = [bank("gate_ps"), bank("up_ps")]
        misc_ps = bank("misc_ps")

        ident = sb("ident", [P, P])
        ident16 = sb("ident16", [P, P], BF16)
        causal16 = sb("causal16", [P, 4, P], BF16)
        zero16 = sb("zero16", [P, 4, P], BF16)
        ones = sb("ones", [P, P])
        ones16 = sb("ones16", [P, 1], BF16)
        exp_of_row = sb("exp_of_row", [NE, P], BF16)
        same16 = sb("same16", [P, P], BF16)
        prior16 = sb("prior16", [P, P], BF16)
        sel_exp = sb("sel_exp", [P, NE], BF16)
        slot_row = sb("slot_row", [P, CAP])
        slot_col = sb("slot_col", [P, SLOT_TILES])
        bits_i = sb("bits_i", [P, TOP_BIT + 1], I32)
        bits_f = sb("bits_f", [P, TOP_BIT + 1])
        exponents = sb("exponents", [P, TOP_BIT + 1], I32)

        x_nat = sb("x_nat", [P, TILES, E])
        stats = sb("stats", [P, TILES, 6])
        mean_var = sb("mean_var", [P, TILES, 2])
        rstd = sb("rstd", [P, TILES])
        var_eps = sb("var_eps", [P, TILES])
        neg_half = sb("neg_half", [P, CT])
        xn = sb("xn", [P, TILES, ROW])
        xnT = sb("xnT", [P, TOKENS])
        wqk_sb = sb("wqk_sb", [P, 2, P])
        bqk_sb = sb("bqk_sb", [P, 2])
        wvg_sb = sb("wvg_sb", [P, ROW])
        bv_sb = sb("bv_sb", [P, E])
        bp_sb = sb("bp_sb", [P, E])
        wp_sb = sb("wp_sb", [P, E])
        qk_f = sb("qk_f", [P, 2, CHUNK])
        qk_rest = sb("qk_rest", [P, 2, CHUNK])
        qk_parts = sb("qk_parts_sb", [P, 2, 2, PARTS, CHUNK], BF16)
        v_nat = sb("v_nat", [P, TILES, E])
        x_bias = sb("x_bias", [P, TILES, E])

        logits = sb("logits", [P, TILES, NE])
        row_max = sb("row_max", [P, TILES])
        shifted = sb("shifted", [P, TILES, NE])
        exped = sb("exped", [P, TILES, NE])
        row_sum = sb("row_sum", [P, TILES])
        row_inv = sb("row_inv", [P, TILES])
        scores = sb("scores", [P, TILES, NE])
        scoresT = sb("scoresT", [P, P])
        cmp = sb("cmp", [P, P])
        count = sb("count", [P, 1], BF16)
        cand = sb("cand", [P, 1], I32)
        cand_next = sb("cand_next", [P, 1], I32)
        reject = sb("reject", [P, 1], I32)
        above = sb("above", [P, P])
        equal = sb("equal", [P, P])
        gt_eq = sb("gt_eq", [P, 2])
        gt_eq16 = sb("gt_eq16", [P, 2], BF16)
        need = sb("need", [P, 1])
        eq_prior = sb("eq_prior", [P, 1])
        eq_rank = sb("eq_rank", [P, P])
        eq_in = sb("eq_in", [P, P])
        eq_kept = sb("eq_kept", [P, P])
        chosen = sb("chosen", [P, P])
        rank = sb("rank", [P, P])
        taken16 = sb("taken16", [P, 1], BF16)
        first = sb("first", [P, 1])
        last = sb("last", [P, 1])
        meta = sb("meta", [P, 3], BF16)
        meta_rest = sb("meta_rest", [P, 1])
        past_first = sb("past_first", [P, CAP])
        in_tile = sb("in_tile", [P, CAP], BF16)
        rank_e = sb("rank_e", [P, NE, P], BF16)
        meta_e = sb("meta_e", [P, NE, 3], BF16)
        slot_meta = sb("slot_meta", [P, SLOT_TILES, NE, 3])
        slot_first = sb("slot_first", [P, SLOT_TILES, NE])
        slot_local = sb("slot_local", [P, SLOT_TILES, NE])
        before = sb("before", [P, SLOT_TILES, P], BF16)
        tok_local = sb("tok_local", [P, NE, SLOT_TILES])
        tok_index = sb("tok_index", [P, NE, SLOT_TILES], U32)

        q_aug = sb("q_aug", [P, 2, HEADS, S], BF16)
        k_aug = sb("k_aug", [P, 2, HEADS, S], BF16)
        v_aug = sb("v_aug", [P, 2, 2, HEADS, 32])
        row_m = sb("row_m", [P, 2, HEADS])
        m_rest = sb("m_rest", [P, 2, HEADS])
        m_parts = sb("m_parts", [P, 2, PARTS, HEADS], BF16)
        mT = sb("mT", [48, S], BF16)
        probs = sb("probs", [P, 6, 512])
        oT = sb("oT", [P, 2, 4, S])
        o_inv = sb("o_inv", [P, HEADS])
        o_nat = sb("o_nat", [P, HEADS, D])
        o_normT = sb("o_normT", [P, P])
        attn = sb("attn", [P, TILES, E])

        w1_sb = sb("w1_sb", [P, 2, HID])
        w3_sb = sb("w3_sb", [P, 2, HID])
        w2_sb = sb("w2_sb", [P, 2, HC, E])
        xg = sb("xg", [P, 2, SLOT_TILES, ROW])
        xg_scaled = sb("xg_scaled", [P, SLOT_TILES, E])
        xgT = sb("xgT", [P, CAP])
        tanh_g = sb("tanh_g", [P, CAP])
        silu2 = sb("silu2", [P, CAP])
        hid = sb("hid", [P, HC, CAP])
        y_sb = sb("y_sb", [P, 2, SLOT_TILES, E])
        sums = sb("sums", [P, TILES, E])
        result = sb("result", [P, TILES, E])

        x_in = [sem(f"x_in{c}") for c in range(CHUNKS)]
        w_in = sem("w_in")
        wp_in = sem("wp_in")
        pool_ready = sem("pool_ready")
        consts_up = sem("consts_up")
        const_ps = sem("const_ps")
        const_sb = sem("const_sb")
        aug_ready = sem("aug_ready")
        stats_up = sem("stats_up")
        mv_up = sem("mv_up")
        var_up = sem("var_up")
        rstd_up = sem("rstd_up")
        xn_up = sem("xn_up")
        xT_ps = sem("xT_ps")
        xT_up = sem("xT_up")
        qk_ps = sem("qk_ps")
        vg_ps = sem("vg_ps")
        q_f_up = sem("q_f_up")
        k_f_up = sem("k_f_up")
        part0_up = sem("part0_up")
        rest_up = sem("rest_up")
        part1_up = sem("part1_up")
        part2_up = sem("part2_up")
        vg_up = sem("vg_up")
        parts_out = [sem(f"parts_out{c}") for c in range(CHUNKS)]
        x_bias_up = sem("x_bias_up")
        acc_out = sem("acc_out")
        gate_step = sem("gate_step")
        bits_up = sem("bits_up")
        gate_exp = sem("gate_exp")
        scores_up = sem("scores_up")
        table_out = sem("table_out")
        scT_ps = sem("scT_ps")
        search = sem("search")
        counted = sem("counted")
        count_ps = sem("count_ps")
        rejected = sem("rejected")
        next_up = sem("next_up")
        pick = sem("pick")
        gt_eq_up = sem("gt_eq_up")
        taken_up = sem("taken_up")
        rank_e_up = sem("rank_e_up")
        before_up = sem("before_up")
        tok_counted = sem("tok_counted")
        pick_ps = sem("pick_ps")
        slots_ps = sem("slots_ps")
        tok_up = sem("tok_up")

        qk_in = [[sem(f"qk_in{b}{hp}") for hp in range(2)] for b in range(2)]
        v_up = sem("v_up")
        nat_full = sem("nat_full")
        nat_max = sem("nat_max")
        m_step = sem("m_step")
        m_in = sem("m_in")
        tr_full = sem("tr_full")
        exp_up = sem("exp_up")
        probs_up = sem("probs_up")
        pv_quads = sem("pv_quads")
        oT_up = sem("oT_up")
        misc_full = sem("misc_full")
        misc_free = sem("misc_free")
        post_step = sem("post_step")
        gathered = [sem("gathered0"), sem("gathered1")]
        ew_in = [sem("ew_in0"), sem("ew_in1")]
        scaled_up = sem("scaled_up")
        ff_full = sem("ff_full")
        tanh_up = sem("tanh_up")
        silu_up = sem("silu_up")
        hid_up = sem("hid_up")
        scattered = sem("scattered")
        sums_in = [sem(f"sums_in{c}") for c in range(CHUNKS)]
        result_up = sem("result_up")
        stored = sem("stored")

        STEPS = 12
        BITS = TOP_BIT + 1
        BITS_AHEAD = 15
        INDEX_BATCH = 1
        EXPERTS = {n: (2 * (n - 2), 2 * (n - 2) + 1) for n in range(2, 2 + NE // 2)}
        NAT_STEPS = (2, 1, 2, 1, 2, 1, 2, 1, 0, 0, 0, 0)

        def bit_at(n, s):
            k = BITS_AHEAD + STEPS * n + s
            return k if k < BITS else None

        def nat_at(s):
            done = sum(NAT_STEPS[:s])
            return range(done, done + NAT_STEPS[s])

        uses = [(-1, "mT")]
        for n in range(B + 1):
            e, before_e = EXPERTS.get(n), EXPERTS.get(n - 1)
            uses += [(n, "x0")] if e else []
            uses += [(n, "y1")] if before_e else []
            uses += [(n, "o0"), (n, "a0"), (n, "pr0")] if n > 0 else []
            uses += [(n, "x1")] if e else []
            uses += [(n, "mT")] if n < B - 1 else []
            uses += [(n, "y0")] if e else []
            uses += [(n, "o1"), (n, "a1"), (n, "pr1")] if n > 0 else []
        MISC = {key: at for at, key in enumerate(uses)}

        block = ctx.enter_context(nc.Block())

        @block.sync
        def _(sp):
            def load_experts(e):
                sp.dma_start(w1_sb[:, e % 2, :], w1[e]).then_inc(ew_in[e % 2], 16)
                sp.dma_start(w3_sb[:, e % 2, :], w3[e]).then_inc(ew_in[e % 2], 16)
                sp.dma_start(w2_sb[:, e % 2], w2[e].rearrange("(c p) n -> p c n", p=P)).then_inc(ew_in[e % 2], 16)

            def load_qk(n, half):
                tok = slice(n * S, (n + 1) * S)
                heads = slice(8 * half, 8 * half + 8)
                for i in range(PARTS):
                    rows = slice(i * PARTS * D, (i + 1) * PARTS * D)
                    q = qk_dram[0, i, half].rearrange("(d h) t -> d h t", d=D)[:, :, tok]
                    sp.dma_start(q_aug[rows, n % 2, heads],
                                 q.unsqueeze(0).broadcast_to([PARTS, D, 8, S])).then_inc(qk_in[n % 2][half], 16)
                    k = qk_dram[1, :, half].rearrange("j (d h) t -> j d h t", d=D)[:, :, :, tok]
                    sp.dma_start(k_aug[rows, n % 2, heads], k).then_inc(qk_in[n % 2][half], 16)

            def load_m(n):
                sp.wait_ge(misc_free, MISC[n - 1, "mT"] + 1)
                sp.dma_start(q_aug[KS:KM, n % 2], mT[:]).then_inc(m_in, 16)

            for c in range(CHUNKS):
                sp.dma_start(x_nat[:, CT * c:CT * c + CT], x_tok[:, CT * c:CT * c + CT]).then_inc(x_in[c], 16)
            sp.dma_start(wqk_sb[:], w_qk).then_inc(w_in, 16)
            sp.dma_start(bqk_sb[:], b_qk).then_inc(w_in, 16)
            sp.dma_start(wvg_sb[:, 0:E], w_v).then_inc(w_in, 16)
            sp.dma_start(wvg_sb[:, E:ROW], w_gate).then_inc(w_in, 16)
            sp.dma_start(bv_sb[:], b_v.partition_broadcast(P)).then_inc(w_in, 16)
            sp.dma_start(bp_sb[:], b_p.partition_broadcast(P)).then_inc(wp_in, 16)
            sp.dma_start(wp_sb[:], w_p).then_inc(wp_in, 16)
            for c in range(CHUNKS):
                sp.wait_ge(part2_up, c + 1)
                for t in range(2):
                    sp.dma_start(qk_dram[t].rearrange("g a r t -> (a r) g t")[:, :, c * CHUNK:(c + 1) * CHUNK],
                                 qk_parts[:, c % 2, t]).then_inc(parts_out[c], 16)
                if c == 0:
                    sp.wait_ge(aug_ready, 1)
                    sp.wait_ge(parts_out[0], 32)
                    load_qk(0, 0)
                    load_qk(0, 1)
            load_qk(1, 0)
            load_qk(1, 1)
            for c in range(1, CHUNKS):
                sp.wait_ge(parts_out[c], 32)
            sp.wait_ge(scores_up, 1)
            sp.dma_start(table.rearrange("(t p) r -> p t r", p=P), xn[:]).then_inc(table_out, 16)
            sp.wait_ge(x_bias_up, 1)
            sp.dma_start(acc.rearrange("(t p) e -> p t e", p=P), x_bias[:]).then_inc(acc_out, 16)
            load_experts(0)
            load_experts(1)
            load_m(0)

            for n in range(B):
                if n + 2 < B:
                    sp.wait_ge(tr_full, STEPS * n + 6)
                    load_qk(n + 2, 0)
                if n in EXPERTS and n - 1 in EXPERTS:
                    sp.wait_ge(misc_full, MISC[n, "y1"] + 1)
                    load_experts(EXPERTS[n][1])
                if n + 1 < B:
                    load_m(n + 1)
                if n + 1 in EXPERTS and n in EXPERTS:
                    sp.wait_ge(misc_full, MISC[n, "y0"] + 1)
                    load_experts(EXPERTS[n + 1][0])
                if n + 2 < B:
                    sp.wait_ge(tr_full, STEPS * n + 12)
                    load_qk(n + 2, 1)
            sp.wait_ge(scattered, 16 * SLOT_TILES * NE)
            for c in range(CHUNKS):
                sp.dma_start(sums[:, CT * c:CT * c + CT],
                             acc.rearrange("(t p) e -> p t e", p=P)[:, CT * c:CT * c + CT]).then_inc(sums_in[c], 16)
            for c in range(CHUNKS):
                sp.wait_ge(result_up, c + 1)
                sp.dma_start(out_tok[:, CT * c:CT * c + CT], result[:, CT * c:CT * c + CT]).then_inc(stored, 16)
            sp.wait_ge(stored, 16 * CHUNKS)

        @block.gpsimd
        def _(pool):
            pool.memset(ones[:], 1.0).then_inc(consts_up, 1)
            pool.memset(ones16[:], 1.0).then_inc(consts_up, 1)
            pool.memset(zero16[:], 0.0).then_inc(consts_up, 1)
            pool.memset(neg_half[:], -0.5).then_inc(consts_up, 1)
            pool.wait_ge(consts_up, 4)
            pool.affine_select(out=ident[:], in_=ones[:], compare_op=ALU.is_equal, fill=0.0, base=0,
                               pattern=[[1, P]], channel_multiplier=-1).then_inc(consts_up, 1)
            pool.affine_select(out=ident16[:], in_=ones[:], compare_op=ALU.is_equal, fill=0.0, base=0,
                               pattern=[[1, P]], channel_multiplier=-1).then_inc(consts_up, 1)
            pool.affine_select(out=exp_of_row[:].rearrange("e (t f) -> e t f", f=NE),
                               in_=ones[0:NE].rearrange("e (t f) -> e t f", f=NE),
                               compare_op=ALU.is_equal, fill=0.0, base=0,
                               pattern=[[0, TILES], [1, NE]], channel_multiplier=-1).then_inc(consts_up, 1)
            for c in range(CHUNKS):
                pool.wait_ge(mv_up, CT * (c + 1))
                pool.tensor_scalar(var_eps[:, CT * c:CT * c + CT], mean_var[:, CT * c:CT * c + CT, 1],
                                   1e-5, None, ALU.add).then_inc(var_up, 1)
                pool.wait_ge(var_up, c + 1)
                pool.tensor_tensor(rstd[:, CT * c:CT * c + CT], var_eps[:, CT * c:CT * c + CT],
                                   neg_half[:], ALU.pow).then_inc(rstd_up, 1)
            pool.affine_select(out=causal16[:], in_=zero16[:], compare_op=ALU.is_ge, fill=MASKED, base=0,
                               pattern=[[0, 4], [-1, P]], channel_multiplier=1).then_inc(consts_up, 1)
            pool.iota(exponents[:], pattern=[[-1, BITS]], base=127 + TOP_BIT,
                      channel_multiplier=0).then_inc(consts_up, 1)
            pool.memset(k_aug[:], -1.0).then_inc(aug_ready, 1)

            def last_part(c):
                pool.wait_ge(part1_up, c + 1)
                pool.tensor_tensor(qk_parts[:, c % 2, :, 2], qk_rest[:], qk_parts[:, c % 2, :, 1],
                                   ALU.subtract).then_inc(part2_up, 1)

            for c in range(CHUNKS):
                last_part(c)
                if c == 0:
                    pool.memset(v_aug[:], 0.0).then_inc(aug_ready, 1)
                    pool.wait_ge(aug_ready, 2)
                    pool.memset(v_aug[:, :, :, :, D:D + 1], 1.0).then_inc(aug_ready, 1)
            pool.iota(slot_row[:], pattern=[[1, CAP]], base=0, channel_multiplier=0,
                      allow_small_or_imprecise_dtypes=True).then_inc(consts_up, 1)
            pool.iota(slot_col[:], pattern=[[P, SLOT_TILES]], base=0, channel_multiplier=1,
                      allow_small_or_imprecise_dtypes=True).then_inc(consts_up, 1)
            pool.wait_ge(const_sb, 2)
            pool.affine_select(out=prior16[:], in_=same16[:], compare_op=ALU.is_gt, fill=0.0, base=0,
                               pattern=[[1, P]], channel_multiplier=-1).then_inc(pool_ready, 1)
            pool.wait_ge(wp_in, 32)
            for c in range(CHUNKS):
                pool.wait_ge(x_in[c], 16)
            pool.tensor_tensor(x_bias[:], x_nat[:], bp_sb[:].unsqueeze(1).broadcast_to([P, TILES, E]),
                               ALU.add).then_inc(x_bias_up, 1)

            def gather(e, tiles):
                pool.wait_ge(tok_up, e + 1)
                pool.wait_ge(table_out, 16)
                if e >= 2:
                    pool.wait_ge(scaled_up, e - 1)
                for s in tiles:
                    pool.indirect_dma_start(
                        out=xg[:, e % 2, s, :], out_offset=None, in_=table[:, :],
                        in_offset=bass.IndirectOffsetOnAxis(ap=tok_index[:, e, s:s + 1], axis=0)
                    ).then_inc(gathered[e % 2], 16)

            def scatter(e, tiles, use):
                pool.wait_ge(misc_free, MISC[use] + 1)
                pool.wait_ge(acc_out, 16)
                if e > 0:
                    pool.wait_ge(scattered, 16 * SLOT_TILES * e)
                for s in tiles:
                    pool.indirect_dma_start(
                        out=acc[:, :], out_offset=bass.IndirectOffsetOnAxis(ap=tok_index[:, e, s:s + 1], axis=0),
                        in_=y_sb[:, e % 2, s, :], in_offset=None, compute_op=ALU.add
                    ).then_inc(scattered, 16)

            def mask_unit(n, s):
                pool.wait_ge(exp_up, STEPS * n + s + 1)
                v = probs[:, s % 6, :]
                if s % 3 < 2:
                    v, heads = v.rearrange("p (h k) -> p h k", h=2)[:, :, 0:P], 2
                else:
                    v, heads = v.rearrange("p (h k) -> p h k", h=4), 4
                pool.affine_select(out=v, in_=v, compare_op=ALU.is_ge, fill=0.0, base=0,
                                   pattern=[[0, heads], [1, P]], channel_multiplier=-1).then_inc(probs_up, 1)

            first_half, second_half = range(SLOT_TILES // 2), range(SLOT_TILES // 2, SLOT_TILES)
            for n in range(B):
                for s in range(STEPS):
                    mask_unit(n, s)
                    if n in EXPERTS and s in (0, 1):
                        gather(EXPERTS[n][1], (first_half, second_half)[s])
                    if n - 1 in EXPERTS and s in (2, 3):
                        scatter(EXPERTS[n - 1][0], (first_half, second_half)[s - 2], (n - 1, "y0"))
                    if n - 1 in EXPERTS and s in (5, 6):
                        scatter(EXPERTS[n - 1][1], (first_half, second_half)[s - 5], (n, "y1"))
                    if n + 1 in EXPERTS and s in (10, 11):
                        gather(EXPERTS[n + 1][0], (first_half, second_half)[s - 10])

        @block.scalar
        def _(act):
            for c in range(CHUNKS):
                act.wait_ge(xT_ps, c + 1)
                act.activation(xnT[:, c * CHUNK:(c + 1) * CHUNK], nat_ps[c % 2][:], ACT.Copy).then_inc(xT_up, 1)
                act.wait_ge(qk_ps, 2 * c + 2)
                if c == 0:
                    act.wait_ge(w_in, 80)
                else:
                    act.wait_ge(rest_up, c)
                act.activation(qk_f[:, 1], tr_ps[1][:], ACT.Identity, bias=bqk_sb[:, 1:2]).then_inc(k_f_up, 1)
                act.wait_ge(k_f_up, c + 1)
                act.wait_ge(q_f_up, c + 1)
                if c >= 2:
                    act.wait_ge(parts_out[c - 2], 32)
                act.activation(qk_parts[:, c % 2, :, 0], qk_f[:], ACT.Copy).then_inc(part0_up, 1)
                act.wait_ge(rest_up, c + 1)
                act.activation(qk_parts[:, c % 2, :, 1], qk_rest[:], ACT.Copy).then_inc(part1_up, 1)
            act.wait_ge(gate_step, 2)
            act.activation(exped[:], shifted[:], ACT.Exp).then_inc(gate_exp, 1)

            def copy_v(n):
                act.activation(v_aug[:, n % 2, :, :, 0:D],
                               v_nat[:, 2 * n:2 * n + 2, :].rearrange("p u (h d) -> p u h d", d=D),
                               ACT.Copy).then_inc(v_up, 1)

            act.wait_ge(vg_up, TILES)
            act.wait_ge(aug_ready, 3)
            copy_v(0)

            def take(use, out, in_):
                act.wait_ge(misc_full, MISC[use] + 1)
                act.activation(out, in_, ACT.Copy).then_inc(misc_free, 1)

            def take_mT(n):
                if n > 0:
                    act.wait_ge(m_in, 16 * n)
                take((n - 1, "mT"), mT[:], misc_ps[:].bitcast(BF16)[0:48, 0:S])

            def take_pr(n, u):
                take((n + 1, f"pr{u}"), attn[:, 2 * n + u, :], misc_ps[:, 0:E])

            def take_y(e, use):
                if e >= 2:
                    act.wait_ge(scattered, 16 * SLOT_TILES * (e - 1))
                take(use, y_sb[:, e % 2], misc_ps[:].rearrange("p (s n) -> p s n", s=SLOT_TILES))

            def exp_unit(n, s):
                act.wait_ge(tr_full, STEPS * n + s + 1)
                if s % 3 == 0 and (n > 0 or s >= 6):
                    act.wait_ge(pv_quads, 4 * n + s // 3 - 1)
                act.activation(probs[:, s % 6, :], tr_ps[s % 2][:], ACT.Exp).then_inc(exp_up, 1)

            def take_o(n, half):
                act.wait_ge(pv_quads, 4 * n + 2 * half + 2)
                if n >= 2:
                    act.wait_ge(misc_full, MISC[n - 1, "o1"] + 1)
                act.activation(oT[:, n % 2, 2 * half:2 * half + 2, :], pv_ps[:].rearrange("p (q t) -> p q t", q=2),
                               ACT.Copy).then_inc(oT_up, 1)

            def tanh(e, c):
                act.wait_ge(ff_full, 4 * e + 2 * c + 1)
                if e > 0 or c > 0:
                    act.wait_ge(silu_up, 2 * e + c)
                act.activation(tanh_g[:], ff_ps[0][:], ACT.Tanh, scale=0.5).then_inc(tanh_up, 1)

            take_mT(0)
            for n in range(B):
                e0, e1 = EXPERTS.get(n, (None, None))
                for s in range(STEPS):
                    exp_unit(n, s)
                    if s == 0 and n - 1 in EXPERTS:
                        tanh(EXPERTS[n - 1][1], 1)
                    if s == 1 and n in EXPERTS:
                        take((n, "x0"), xgT[:], misc_ps[:])
                    if s == 2:
                        if n > 0:
                            take_o(n - 1, 1)
                        if n - 1 in EXPERTS:
                            take_y(EXPERTS[n - 1][1], (n, "y1"))
                    if s == 3 and n in EXPERTS:
                        tanh(e0, 0)
                    if s == 5 and n > 0:
                        take((n, "a0"), o_normT[:], misc_ps[:, 0:P])
                    if s == 6:
                        if n > 0:
                            take_pr(n - 1, 0)
                        if n in EXPERTS:
                            tanh(e0, 1)
                    if s == 7 and n in EXPERTS:
                        take((n, "x1"), xgT[:], misc_ps[:])
                    if s == 8:
                        take_o(n, 0)
                        if n < B - 1:
                            take_mT(n + 1)
                        if n in EXPERTS:
                            take_y(e0, (n, "y0"))
                    if s == 9:
                        if n < B - 1:
                            act.wait_ge(pv_quads, 4 * n)
                            copy_v(n + 1)
                        if n in EXPERTS:
                            tanh(e1, 0)
                    if s == 10 and n > 0:
                        take((n, "a1"), o_normT[:], misc_ps[:, 0:P])
                    if s == 11 and n > 0:
                        take_pr(n - 1, 1)
            take_o(B - 1, 1)
            for u in range(2):
                take((B, f"a{u}"), o_normT[:], misc_ps[:, 0:P])
                take_pr(B - 1, u)

        @block.vector
        def _(dve):
            for c in range(CHUNKS):
                dve.wait_ge(x_in[c], 16)
                for t in range(CT * c, CT * c + CT):
                    dve.bn_stats(stats[:, t, :], x_nat[:, t, :]).then_inc(stats_up, 1)
                for t in range(CT * c, CT * c + CT):
                    dve.wait_ge(stats_up, t + 1)
                    dve.bn_aggr(mean_var[:, t, :], stats[:, t, :]).then_inc(mv_up, 1)

            def normalize(c):
                dve.wait_ge(rstd_up, c + 1)
                for t in range(CT * c, CT * c + CT):
                    dve.tensor_scalar(xn[:, t, 0:E], x_nat[:, t, :], mean_var[:, t, 0:1], rstd[:, t:t + 1],
                                      ALU.subtract, ALU.mult).then_inc(xn_up, 1)

            def take_qk(c):
                if c == 0:
                    dve.wait_ge(w_in, 80)
                dve.wait_ge(qk_ps, 2 * c + 1)
                dve.tensor_scalar(qk_f[:, 0], tr_ps[0][:], bqk_sb[:, 0:1], INV_SQRT_D,
                                  ALU.add, ALU.mult).then_inc(q_f_up, 1)

            def rest(c):
                dve.wait_ge(part0_up, c + 1)
                if c > 0:
                    dve.wait_ge(part2_up, c)
                dve.tensor_tensor(qk_rest[:], qk_f[:], qk_parts[:, c % 2, :, 0], ALU.subtract).then_inc(rest_up, 1)

            def take_vg(c):
                for u in range(2):
                    dve.wait_ge(vg_ps, 2 * c + u + 1)
                    t = CT * c + 2 * u
                    ps = ff_ps[u][:, 0:2 * ROW].rearrange("p (t r) -> p t r", t=2)
                    dve.tensor_tensor(v_nat[:, t:t + 2, :], ps[:, :, 0:E],
                                      bv_sb[:].unsqueeze(1).broadcast_to([P, 2, E]), ALU.add).then_inc(vg_up, 1)
                    dve.tensor_copy(logits[:, t:t + 2, :], ps[:, :, E:ROW]).then_inc(vg_up, 1)

            normalize(0)
            dve.wait_ge(const_ps, 1)
            dve.tensor_copy(same16[:], misc_ps[:, 0:P]).then_inc(const_sb, 1)
            dve.tensor_copy(sel_exp[:], misc_ps[:, P:P + NE]).then_inc(const_sb, 1)
            for c in range(CHUNKS):
                if c + 1 < CHUNKS:
                    normalize(c + 1)
                take_qk(c)
                rest(c)
                take_vg(c)

            dve.wait_ge(consts_up, 9)
            dve.tensor_scalar(bits_f[:].bitcast(I32), exponents[:], 23, None,
                              ALU.logical_shift_left).then_inc(bits_up, 1)
            dve.memset(cand[:], CAND_START).then_inc(bits_up, 1)
            dve.wait_ge(bits_up, 2)
            dve.tensor_copy(bits_i[:], bits_f[:]).then_inc(bits_up, 1)

            def spread(a):
                return a[:].unsqueeze(2).broadcast_to([P, TILES, NE])

            dve.wait_ge(vg_up, TILES)
            dve.tensor_reduce(row_max[:], logits[:], AX_X, ALU.max).then_inc(gate_step, 1)
            dve.wait_ge(gate_step, 1)
            dve.tensor_tensor(shifted[:], logits[:], spread(row_max), ALU.subtract).then_inc(gate_step, 1)
            dve.wait_ge(gate_exp, 1)
            dve.tensor_reduce(row_sum[:], exped[:], AX_X, ALU.add).then_inc(gate_step, 1)
            dve.wait_ge(gate_step, 3)
            dve.reciprocal(row_inv[:], row_sum[:]).then_inc(gate_step, 1)
            dve.wait_ge(gate_step, 4)
            dve.tensor_tensor(scores[:], exped[:], spread(row_inv), ALU.mult).then_inc(gate_step, 1)
            dve.wait_ge(gate_step, 5)
            dve.tensor_copy(xn[:, :, E:ROW], scores[:]).then_inc(scores_up, 1)
            dve.wait_ge(scT_ps, 1)
            dve.tensor_copy(scoresT[:], misc_ps[:, 0:P]).then_inc(search, 1)
            dve.wait_ge(bits_up, 3)

            def try_bit(k):
                dve.wait_ge(search, k + 1)
                dve.tensor_scalar(cmp[:], scoresT[:], cand[:].bitcast(F32), 0.0, ALU.is_ge, ALU.add,
                                  accum_out=count[:]).then_inc(counted, 1)
                if k + 1 < BITS:
                    dve.tensor_tensor(cand_next[:], cand[:], bits_i[:, k + 1:k + 2],
                                      ALU.bitwise_or).then_inc(next_up, 1)

            def settle_bit(k):
                dve.wait_ge(count_ps, k + 1)
                dve.scalar_tensor_tensor(out=reject[:], in0=ff_ps[1][:, 0:1], scalar=CAP - 0.5,
                                         in1=bits_f[:, k:k + 1], op0=ALU.is_lt, op1=ALU.mult).then_inc(rejected, 1)
                dve.wait_ge(rejected, k + 1)
                if k + 1 < BITS:
                    dve.wait_ge(next_up, k + 1)
                    base = cand_next
                else:
                    base = cand
                dve.tensor_tensor(cand[:], base[:], reject[:], ALU.bitwise_xor).then_inc(search, 1)

            def search_step(k):
                if k is not None:
                    if k > 0:
                        settle_bit(k - 1)
                    try_bit(k)

            picks = [0]

            def link(ins):
                picks[0] += 1
                ins.then_inc(pick, 1)
                dve.wait_ge(pick, picks[0])

            def mark_tokens():
                settle_bit(BITS - 1)
                dve.wait_ge(search, BITS + 1)
                limit = cand[:].bitcast(F32)
                link(dve.tensor_scalar(above[:], scoresT[:], limit, 0.0, ALU.is_gt, ALU.add,
                                       accum_out=gt_eq[:, 0:1]))
                link(dve.tensor_scalar(equal[:], scoresT[:], limit, 0.0, ALU.is_equal, ALU.add,
                                       accum_out=gt_eq[:, 1:2]))
                dve.tensor_copy(gt_eq16[:], gt_eq[:]).then_inc(gt_eq_up, 1)

            def rank_tokens():
                dve.wait_ge(pick_ps, 1)
                link(dve.tensor_scalar(need[:], ff_ps[1][:, 0:1], -1.0, float(CAP), ALU.mult, ALU.add))
                link(dve.tensor_copy(eq_prior[:], ff_ps[1][:, 1:2]))
                link(dve.tensor_tensor_scan(eq_rank[:], ones[:], equal[:], eq_prior[:], ALU.mult, ALU.add))
                link(dve.scalar_tensor_tensor(out=eq_kept[:], in0=eq_rank[:], scalar=need[:], in1=equal[:],
                                              op0=ALU.is_le, op1=ALU.mult))
                link(dve.tensor_tensor(chosen[:], above[:], eq_kept[:], ALU.add))
                link(dve.tensor_tensor_scan(rank[:], ones[:], chosen[:], 0.0, ALU.mult, ALU.add))
                dve.tensor_copy(taken16[:], rank[:, P - 1:P]).then_inc(taken_up, 1)

            def place_rows():
                dve.wait_ge(pick_ps, 2)
                dve.wait_ge(consts_up, 11)
                link(dve.tensor_copy(first[:], ff_ps[1][:, 0:1]))
                link(dve.tensor_copy(meta[:, 0:1], ff_ps[1][:, 1:2]))
                link(dve.tensor_tensor(last[:], first[:], rank[:, P - 1:P], ALU.add))
                link(dve.tensor_copy(meta[:, 1:2], first[:]))
                link(dve.tensor_tensor(meta[:, 2:3], first[:], meta[:, 1:2], ALU.subtract))
                link(dve.tensor_scalar(past_first[:], slot_row[:], first[:], None, ALU.is_ge))

            def spread_rows():
                link(dve.scalar_tensor_tensor(out=in_tile[:], in0=slot_row[:], scalar=last[:], in1=past_first[:],
                                              op0=ALU.is_lt, op1=ALU.mult))
                link(dve.tensor_tensor(meta_e[:], meta[:].unsqueeze(1).broadcast_to([P, NE, 3]),
                                       sel_exp[:].unsqueeze(2).broadcast_to([P, NE, 3]), ALU.mult))
                dve.tensor_tensor(rank_e[:], rank[:].unsqueeze(1).broadcast_to([P, NE, P]),
                                  sel_exp[:].unsqueeze(2).broadcast_to([P, NE, P]), ALU.mult).then_inc(rank_e_up, 1)

            def take_meta():
                dve.wait_ge(slots_ps, 1)
                link(dve.tensor_copy(slot_meta[:], ff_ps[0][:, 0:SLOT_TILES * NE * 3].rearrange(
                    "p (s e m) -> p s e m", s=SLOT_TILES, e=NE)))
                link(dve.tensor_tensor(slot_first[:], slot_meta[:, :, :, 1], slot_meta[:, :, :, 2], ALU.add))
                link(dve.tensor_tensor(slot_local[:], slot_col[:].unsqueeze(2).broadcast_to([P, SLOT_TILES, NE]),
                                       slot_first[:], ALU.subtract))

            def find_tokens(e):
                dve.wait_ge(slots_ps, e + 2)
                dve.tensor_tensor(before[:], nat_ps[e % 2][:].rearrange("p (s t) -> p s t", s=SLOT_TILES),
                                  slot_local[:, :, e:e + 1].broadcast_to([P, SLOT_TILES, P]),
                                  ALU.is_le).then_inc(before_up, 1)
                dve.wait_ge(before_up, e + 1)
                dve.tensor_reduce(tok_local[:, e, :], before[:], AX_X, ALU.add).then_inc(tok_counted, 1)
                dve.wait_ge(tok_counted, e + 1)
                dve.scalar_tensor_tensor(out=tok_index[:, e, :], in0=slot_meta[:, :, e, 0], scalar=float(P),
                                         in1=tok_local[:, e, :], op0=ALU.mult, op1=ALU.add).then_inc(tok_up, 1)

            def max_unit(n, v):
                q, j = v // 3, v % 3
                dve.wait_ge(nat_full, STEPS * n + v + 1)
                if j == 0:
                    dst, heads = row_m[:, 0, 4 * q:4 * q + 4], 4
                else:
                    h = 4 * q + 2 * (j - 1)
                    dst, heads = row_m[:, 1, h:h + 2], 2
                dve.tensor_reduce(dst, nat_ps[v % 2][:].rearrange("p (h k) -> p h k", h=heads),
                                  AX_X, ALU.max).then_inc(nat_max, 1)

            def split_m(n):
                dve.wait_ge(nat_max, STEPS * n + 12)
                dve.tensor_copy(m_parts[:, :, 0, :], row_m[:]).then_inc(m_step, 1)
                dve.wait_ge(m_step, 4 * n + 1)
                dve.tensor_tensor(m_rest[:], row_m[:], m_parts[:, :, 0, :], ALU.subtract).then_inc(m_step, 1)
                dve.wait_ge(m_step, 4 * n + 2)
                dve.tensor_copy(m_parts[:, :, 1, :], m_rest[:]).then_inc(m_step, 1)
                dve.wait_ge(m_step, 4 * n + 3)
                dve.tensor_tensor(m_parts[:, :, 2, :], m_rest[:], m_parts[:, :, 1, :],
                                  ALU.subtract).then_inc(m_step, 1)

            for v in range(STEPS):
                search_step(v)
                max_unit(0, v)
            split_m(0)
            for k in range(STEPS, BITS_AHEAD):
                search_step(k)

            def scale_rows(e):
                dve.wait_ge(gathered[e % 2], 16 * SLOT_TILES * (e // 2 + 1))
                if e > 0:
                    dve.wait_ge(misc_full, MISC[next((n, f"x{i}") for n, es in EXPERTS.items()
                                                     for i in range(2) if es[i] == e - 1)] + 1)
                dve.tensor_tensor(xg_scaled[:], xg[:, e % 2, :, 0:E],
                                  xg[:, e % 2, :, E + e:E + e + 1].broadcast_to([P, SLOT_TILES, E]),
                                  ALU.mult).then_inc(scaled_up, 1)

            def take_o(n, u):
                o = misc_ps[:].rearrange("p (h r) -> p h r", r=32)
                dve.wait_ge(misc_full, MISC[n + 1, f"o{u}"] + 1)
                dve.reciprocal(o_inv[:], o[:, :, D]).then_inc(post_step, 1)
                dve.wait_ge(post_step, 2 * n + u + 1)
                dve.tensor_tensor(o_nat[:], o[:, :, 0:D], o_inv[:].unsqueeze(2).broadcast_to([P, HEADS, D]),
                                  ALU.mult).then_inc(misc_free, 1)

            def gated(e, c):
                dve.wait_ge(tanh_up, 2 * e + c + 1)
                dve.scalar_tensor_tensor(out=silu2[:], in0=tanh_g[:], scalar=1.0, in1=ff_ps[0][:],
                                         op0=ALU.add, op1=ALU.mult).then_inc(silu_up, 1)
                dve.wait_ge(silu_up, 2 * e + c + 1)
                dve.wait_ge(ff_full, 4 * e + 2 * c + 2)
                dve.scalar_tensor_tensor(out=hid[:, c, :], in0=silu2[:], scalar=0.5, in1=ff_ps[1][:],
                                         op0=ALU.mult, op1=ALU.mult).then_inc(hid_up, 1)

            for n in range(B):
                e0, e1 = EXPERTS.get(n, (None, None))
                for s in range(STEPS):
                    search_step(bit_at(n, s))
                    if s == 1 and n - 1 in EXPERTS:
                        gated(EXPERTS[n - 1][1], 1)
                    if s == 4 and n in EXPERTS:
                        gated(e0, 0)
                    if s == 7 and n in EXPERTS:
                        gated(e0, 1)
                    if s == 10 and n in EXPERTS:
                        gated(e1, 0)
                    if n < B - 1:
                        for v in nat_at(s):
                            max_unit(n + 1, v)
                    if s == 0 and n in EXPERTS:
                        scale_rows(e0)
                    if s == 3 and n > 0:
                        take_o(n - 1, 0)
                    if s == 5 and n in EXPERTS:
                        scale_rows(e1)
                    if s == 7 and n < B - 1:
                        split_m(n + 1)
                    if s == 9 and n > 0:
                        take_o(n - 1, 1)
                    if n == INDEX_BATCH:
                        if s == 3:
                            mark_tokens()
                        if s == 4:
                            rank_tokens()
                        if s == 6:
                            place_rows()
                        if s == 7:
                            spread_rows()
                        if s == 9:
                            take_meta()
                    if n + 1 in EXPERTS and s in (9, 10):
                        find_tokens(EXPERTS[n + 1][s - 9])
            for u in range(2):
                take_o(B - 1, u)
            for c in range(CHUNKS):
                dve.wait_ge(sums_in[c], 16)
                dve.wait_ge(misc_free, MISC[2 * c + 2, "pr1"] + 1)
                dve.tensor_tensor(result[:, CT * c:CT * c + CT], attn[:, CT * c:CT * c + CT],
                                  sums[:, CT * c:CT * c + CT], ALU.add).then_inc(result_up, 1)

        @block.tensor
        def _(pe):
            pe.wait_ge(consts_up, 7)
            pe.matmul(misc_ps[:, 0:P], exp_of_row[:], exp_of_row[:], start=True, stop=True)
            pe.matmul(misc_ps[:, P:P + NE], exp_of_row[:], ident16[0:NE, 0:NE], start=True,
                      stop=True).then_inc(const_ps, 1)

            def turn_x(c):
                pe.wait_ge(xn_up, CT * c + CT)
                if c >= 2:
                    pe.wait_ge(xT_up, c - 1)
                for u in range(CT):
                    ins = pe.transpose(nat_ps[c % 2][:, u * P:(u + 1) * P], xn[:, CT * c + u, 0:E], ident[:])
                ins.then_inc(xT_ps, 1)

            turn_x(0)
            for c in range(CHUNKS):
                if c + 1 < CHUNKS:
                    turn_x(c + 1)
                pe.wait_ge(xT_up, c + 1)
                if c == 0:
                    pe.wait_ge(w_in, 80)
                else:
                    pe.wait_ge(q_f_up, c)
                    pe.wait_ge(k_f_up, c)
                for t in range(2):
                    pe.matmul(tr_ps[t][:], wqk_sb[:, t, :], xnT[:, c * CHUNK:(c + 1) * CHUNK],
                              start=True, stop=True).then_inc(qk_ps, 1)
                if c > 0:
                    pe.wait_ge(vg_up, CT * c)
                for u in range(2):
                    for v in range(2):
                        t = CT * c + 2 * u + v
                        ins = pe.matmul(ff_ps[u][:, v * ROW:(v + 1) * ROW], xnT[:, t * P:(t + 1) * P], wvg_sb[:],
                                        start=True, stop=True)
                    ins.then_inc(vg_ps, 1)

            pe.wait_ge(const_sb, 2)
            pe.wait_ge(scores_up, 1)
            pe.transpose(misc_ps[:, 0:P], scores[:].rearrange("p t e -> p (t e)"), ident[:]).then_inc(scT_ps, 1)

            def count_bit(k):
                if k is not None:
                    pe.wait_ge(counted, k + 1)
                    pe.matmul(ff_ps[1][:, 0:1], same16[:], count[:], start=True, stop=True).then_inc(count_ps, 1)

            def count_marked():
                pe.wait_ge(gt_eq_up, 1)
                pe.wait_ge(pool_ready, 1)
                pe.matmul(ff_ps[1][:, 0:1], same16[:], gt_eq16[:, 0:1], start=True, stop=True)
                pe.matmul(ff_ps[1][:, 1:2], prior16[:], gt_eq16[:, 1:2], start=True, stop=True).then_inc(pick_ps, 1)

            def count_taken():
                pe.wait_ge(taken_up, 1)
                pe.matmul(ff_ps[1][:, 0:1], prior16[:], taken16[:], start=True, stop=True)
                pe.matmul(ff_ps[1][:, 1:2], prior16[:], ones16[:], start=True, stop=True).then_inc(pick_ps, 1)

            def slot_rows():
                pe.wait_ge(rank_e_up, 1)
                for s in range(SLOT_TILES):
                    ins = pe.matmul(ff_ps[0][:, s * NE * 3:(s + 1) * NE * 3], in_tile[:, s * P:(s + 1) * P],
                                    meta_e[:].rearrange("p e m -> p (e m)"), start=True, stop=True)
                ins.then_inc(slots_ps, 1)

            def slot_ranks(e, n):
                pe.wait_ge(nat_max, STEPS * (n + 1))
                for s in range(SLOT_TILES):
                    ins = pe.matmul(nat_ps[e % 2][:, s * P:(s + 1) * P], in_tile[:, s * P:(s + 1) * P],
                                    rank_e[:, e, :], start=True, stop=True)
                ins.then_inc(slots_ps, 1)

            def nat_unit(n, v):
                q, j = v // 3, v % 3
                p = n % 2
                ps = nat_ps[v % 2]
                if v in (0, 6):
                    pe.wait_ge(qk_in[p][q // 2], 96 * (n // 2 + 1))
                if n > 0 or v >= 2:
                    pe.wait_ge(nat_max, STEPS * n + v - 1)
                if v < 2 and n - 1 in EXPERTS:
                    pe.wait_ge(before_up, EXPERTS[n - 1][v] + 1)
                if j == 0:
                    pe.matmul(ps[:], ident16[:], causal16[:].rearrange("p a k -> p (a k)"), start=True, stop=False,
                              skip_group_check=True)
                    for c in range(4):
                        h = 4 * q + c
                        ins = pe.matmul(ps[:, c * P:(c + 1) * P], q_aug[0:KS, p, h, 0:P], k_aug[0:KS, p, h, 0:P],
                                        start=False, stop=True, skip_group_check=True)
                else:
                    pe.matmul(ps[:].rearrange("p (h k) -> p h k", h=2)[:, :, P:S], ident16[:], causal16[:, 0:2, :],
                              start=True, stop=False, skip_group_check=True)
                    for c in range(2):
                        h = 4 * q + 2 * (j - 1) + c
                        ins = pe.matmul(ps[:, c * S:(c + 1) * S], q_aug[0:KS, p, h, P:S], k_aug[0:KS, p, h, 0:S],
                                        start=False, stop=True, skip_group_check=True)
                ins.then_inc(nat_full, 1)

            def tr_unit(n, s):
                q, j = s // 3, s % 3
                p = n % 2
                ps = tr_ps[s % 2]
                if s == 0:
                    pe.wait_ge(m_in, 16 * (n + 1))
                if n > 0 or s >= 2:
                    pe.wait_ge(exp_up, STEPS * n + s - 1)
                if j < 2:
                    for c in range(2):
                        h = 4 * q + 2 * j + c
                        ins = pe.matmul(ps[:, c * S:(c + 1) * S], k_aug[0:KM, p, h, 0:P], q_aug[0:KM, p, h, :],
                                        start=True, stop=True)
                else:
                    for c in range(4):
                        h = 4 * q + c
                        ins = pe.matmul(ps[:, c * P:(c + 1) * P], k_aug[0:KM, p, h, P:S], q_aug[0:KM, p, h, P:S],
                                        start=True, stop=True)
                ins.then_inc(tr_full, 1)

            def pv(n, q):
                pe.wait_ge(probs_up, STEPS * n + 3 * q + 3)
                if q == 0:
                    pe.wait_ge(v_up, n + 1)
                if q % 2 == 0 and (n > 0 or q > 0):
                    pe.wait_ge(oT_up, 2 * n + q // 2)
                col = (q % 2) * S
                for c in range(4):
                    pe.matmul(pv_ps[32 * c:32 * c + 32, col:col + S], v_aug[:, n % 2, 0, 4 * q + c, :],
                              probs[:, (3 * q + c // 2) % 6, (c % 2) * S:(c % 2) * S + S], start=True, stop=False,
                              tile_position=(0, 32 * c), skip_group_check=True)
                for c in range(4):
                    ins = pe.matmul(pv_ps[32 * c:32 * c + 32, col + P:col + S], v_aug[:, n % 2, 1, 4 * q + c, :],
                                    probs[:, (3 * q + 2) % 6, c * P:(c + 1) * P], start=False, stop=True,
                                    tile_position=(0, 32 * c), skip_group_check=True)
                ins.then_inc(pv_quads, 1)

            def use(key):
                if MISC[key] > 0:
                    pe.wait_ge(misc_free, MISC[key])

            def turn_m(n):
                pe.wait_ge(m_step, 4 * n + 4)
                use((n - 1, "mT"))
                for u in range(2):
                    ins = pe.transpose(misc_ps[:].bitcast(BF16)[0:48, u * P:(u + 1) * P],
                                       m_parts[:, u].rearrange("p s h -> p (s h)"), ident16[:])
                ins.then_inc(misc_full, 1)

            def turn_rows(e, key):
                pe.wait_ge(scaled_up, e + 1)
                use(key)
                for s in range(SLOT_TILES):
                    ins = pe.transpose(misc_ps[:, s * P:(s + 1) * P], xg_scaled[:, s, :], ident[:])
                ins.then_inc(misc_full, 1)

            def gate_up(e, c, key):
                if c == 0:
                    pe.wait_ge(misc_free, MISC[key] + 1)
                    pe.wait_ge(ew_in[e % 2], 48 * (e // 2 + 1))
                if e > 0 or c > 0:
                    pe.wait_ge(hid_up, 2 * e + c)
                pe.matmul(ff_ps[0][:], w1_sb[:, e % 2, c * P:(c + 1) * P], xgT[:], start=True, stop=True
                          ).then_inc(ff_full, 1)
                pe.matmul(ff_ps[1][:], w3_sb[:, e % 2, c * P:(c + 1) * P], xgT[:], start=True, stop=True
                          ).then_inc(ff_full, 1)

            def down(e, key):
                pe.wait_ge(hid_up, 2 * e + 2)
                use(key)
                for s in range(SLOT_TILES):
                    for c in range(HC):
                        ins = pe.matmul(misc_ps[:, s * P:(s + 1) * P], hid[:, c, s * P:(s + 1) * P],
                                        w2_sb[:, e % 2, c, :], start=(c == 0), stop=(c == HC - 1))
                ins.then_inc(misc_full, 1)

            def turn_o(n, u):
                pe.wait_ge(oT_up, 2 * n + 2)
                use((n + 1, f"o{u}"))
                for q in range(4):
                    ins = pe.transpose(misc_ps[:, q * P:(q + 1) * P], oT[:, n % 2, q, u * P:(u + 1) * P], ident[:])
                ins.then_inc(misc_full, 1)

            def turn_a(n, u):
                use((n + 1, f"a{u}"))
                pe.transpose(misc_ps[:, 0:P], o_nat[:].rearrange("p h d -> p (h d)"), ident[:]).then_inc(misc_full, 1)

            def project(n, u):
                use((n + 1, f"pr{u}"))
                pe.matmul(misc_ps[:, 0:E], o_normT[:], wp_sb[:], start=True, stop=True).then_inc(misc_full, 1)

            pe.wait_ge(consts_up, 8)
            pe.wait_ge(wp_in, 32)
            pe.wait_ge(search, 1)
            for v in range(STEPS):
                nat_unit(0, v)
                count_bit(v)
            for k in range(STEPS, BITS_AHEAD):
                if k == STEPS:
                    turn_m(0)
                count_bit(k)

            for n in range(B):
                e0, e1 = EXPERTS.get(n, (None, None))
                for s in range(STEPS):
                    tr_unit(n, s)
                    if n < B - 1:
                        for v in nat_at(s):
                            nat_unit(n + 1, v)
                    count_bit(bit_at(n, s))
                    if s == 0 and n - 1 in EXPERTS:
                        gate_up(EXPERTS[n - 1][1], 1, None)
                    if s == 1:
                        if n > 0:
                            pv(n - 1, 3)
                        if n in EXPERTS:
                            turn_rows(e0, (n, "x0"))
                    if s == 2 and n - 1 in EXPERTS:
                        down(EXPERTS[n - 1][1], (n, "y1"))
                    if s == 3:
                        if n > 0:
                            turn_o(n - 1, 0)
                        if n in EXPERTS:
                            gate_up(e0, 0, (n, "x0"))
                    if s == 4:
                        pv(n, 0)
                    if s == 5 and n > 0:
                        turn_a(n - 1, 0)
                    if s == 6:
                        if n > 0:
                            project(n - 1, 0)
                        if n in EXPERTS:
                            gate_up(e0, 1, None)
                    if s == 7:
                        pv(n, 1)
                        if n in EXPERTS:
                            turn_rows(e1, (n, "x1"))
                    if s == 8:
                        if n < B - 1:
                            turn_m(n + 1)
                        if n in EXPERTS:
                            down(e0, (n, "y0"))
                        if n == INDEX_BATCH:
                            slot_rows()
                        if n + 1 in EXPERTS:
                            for e in EXPERTS[n + 1]:
                                slot_ranks(e, n + 1)
                    if s == 9:
                        if n > 0:
                            turn_o(n - 1, 1)
                        if n in EXPERTS:
                            gate_up(e1, 0, (n, "x1"))
                    if s == 10:
                        pv(n, 2)
                        if n > 0:
                            turn_a(n - 1, 1)
                    if s == 11 and n > 0:
                        project(n - 1, 1)
                    if n == INDEX_BATCH:
                        if s == 3:
                            count_marked()
                        if s == 5:
                            count_taken()
            pv(B - 1, 3)
            for u in range(2):
                turn_o(B - 1, u)
                turn_a(B - 1, u)
                project(B - 1, u)


def kernel(**inputs):
    import numpy as np
    import concourse.bacc as bacc
    from concourse import mybir as _mybir
    from concourse.bass_utils import run_bass_kernel_spmd as run

    x = np.ascontiguousarray(inputs["L0_attn_x"])
    E = x.shape[-1]
    w = np.asarray(inputs["L0_attn_W1"]).reshape(E, 2, HEADS // 2, 3, E // HEADS)
    b = np.asarray(inputs["L0_attn_b1"]).reshape(2, HEADS // 2, 3, E // HEADS)
    arrays = {
        "x": x,
        "w_qk": w[:, :, :, 0:2].transpose(0, 3, 1, 4, 2).reshape(E, 2, E),
        "b_qk": b[:, :, 0:2].transpose(0, 3, 1, 2).reshape(E, 2),
        "w_v": w[:, :, :, 2].reshape(E, E),
        "b_v": b[:, :, 2].reshape(E),
        "w_p": np.asarray(inputs["L0_attn_Wp"]),
        "b_p": np.asarray(inputs["L0_attn_bp"]),
        "w_gate": np.asarray(inputs["L0_ffn_wg"]),
        "w1": np.asarray(inputs["L0_ffn_w1"]),
        "w3": np.asarray(inputs["L0_ffn_w3"]),
        "w2": np.asarray(inputs["L0_ffn_w2"]),
    }
    arrays = {k: np.ascontiguousarray(v) for k, v in arrays.items()}
    nc = bacc.Bacc("TRN2", target_bir_lowering=False, num_devices=1)
    args = [nc.dram_tensor(k, v.shape, _mybir.dt.from_np(v.dtype), kind="ExternalInput").ap()
            for k, v in arrays.items()]
    out = nc.dram_tensor("out", x.shape, _mybir.dt.from_np(x.dtype), kind="ExternalOutput").ap()
    attention_moe_block(nc, *args, out)
    r = run(nc, [arrays], core_ids=[0])
    return r.results[0]["out"]
```

```python
from contextlib import ExitStack

import concourse.bass as bass
from concourse import mybir

ALU = mybir.AluOpType
ACT = mybir.ActivationFunctionType
F32 = mybir.dt.float32
BF16 = mybir.dt.bfloat16
I32 = mybir.dt.int32
U32 = mybir.dt.uint32
AX_X = mybir.AxisListType.X

P = 128
HEADS = 16
TOP_BIT = 29
CAND_START = 1 << TOP_BIT


def attention_moe_block(nc, x, w_qk, b_qk, w_v, b_v, w_p, b_p, w_gate, w1, w3, w2, out):
    B, S, E = x.shape
    NE, _, HID = w1.shape
    TOKENS = B * S
    TILES = TOKENS // P
    CAP = TOKENS // 4
    SLOT_TILES = CAP // P
    HC = HID // P
    D = E // HEADS
    CHUNK = 512
    CT = CHUNK // P
    CHUNKS = TOKENS // CHUNK
    PARTS = 3
    KS = PARTS * PARTS * D
    KM = KS + PARTS
    ROW = E + NE
    INV_SQRT_D = float(D) ** -0.5
    MASKED = -1.0e6
    assert E == P and S == 2 * P and NE == B and HEADS == 16 and CAP == CHUNK and TILES * NE == P

    x_tok = x.rearrange("b (u p) e -> p (b u) e", p=P)
    out_tok = out.rearrange("b (u p) e -> p (b u) e", p=P)

    with ExitStack() as ctx:
        def sb(name, shape, dt=F32):
            return ctx.enter_context(nc.sbuf_tensor(name, shape, dt))

        def bank(name):
            return ctx.enter_context(nc.psum_tensor(name, [P, 512], F32))

        def sem(name):
            return ctx.enter_context(nc.semaphore(name))

        table = nc.dram_tensor("token_table", (TOKENS, ROW), F32).ap()
        acc = nc.dram_tensor("expert_sum", (TOKENS, E), F32).ap()
        qk_dram = nc.dram_tensor("qk_parts", (2, PARTS, 2, P // 2, TOKENS), BF16).ap()

        nat_ps = [bank("nat_ps0"), bank("nat_ps1")]
        tr_ps = [bank("tr_ps0"), bank("tr_ps1")]
        pv_ps = bank("pv_ps")
        ff_ps = [bank("gate_ps"), bank("up_ps")]
        misc_ps = bank("misc_ps")

        ident = sb("ident", [P, P])
        ident16 = sb("ident16", [P, P], BF16)
        causal16 = sb("causal16", [P, 4, P], BF16)
        zero16 = sb("zero16", [P, 4, P], BF16)
        keep = sb("keep", [P, P])
        ones = sb("ones", [P, P])
        ones16 = sb("ones16", [P, 1], BF16)
        exp_of_row = sb("exp_of_row", [NE, P], BF16)
        same16 = sb("same16", [P, P], BF16)
        prior16 = sb("prior16", [P, P], BF16)
        sel_exp = sb("sel_exp", [P, NE], BF16)
        slot_row = sb("slot_row", [P, CAP])
        slot_col = sb("slot_col", [P, SLOT_TILES])
        bits_i = sb("bits_i", [P, TOP_BIT + 1], I32)
        bits_f = sb("bits_f", [P, TOP_BIT + 1])
        exponents = sb("exponents", [P, TOP_BIT + 1], I32)

        x_nat = sb("x_nat", [P, TILES, E])
        stats = sb("stats", [P, TILES, 6])
        mean_var = sb("mean_var", [P, TILES, 2])
        rstd = sb("rstd", [P, TILES])
        var_eps = sb("var_eps", [P, TILES])
        neg_half = sb("neg_half", [P, CT])
        neg_ones = sb("neg_ones", [PARTS, S], BF16)
        xn = sb("xn", [P, TILES, ROW])
        xnT = sb("xnT", [P, TOKENS])
        wqk_sb = sb("wqk_sb", [P, 2, P])
        bqk_sb = sb("bqk_sb", [P, 2])
        bq_scaled = sb("bq_scaled", [P, 1])
        wvg_sb = sb("wvg_sb", [P, ROW])
        bv_sb = sb("bv_sb", [P, E])
        bp_sb = sb("bp_sb", [P, E])
        wp_sb = sb("wp_sb", [P, E])
        qk_f = sb("qk_f", [P, 2, 2, CHUNK])
        qk_rest = sb("qk_rest", [P, 2, 2, CHUNK])
        qk_parts = sb("qk_parts_sb", [P, CHUNKS, 2, PARTS, CHUNK], BF16)
        v_nat = sb("v_nat", [P, TILES, E])
        x_bias = sb("x_bias", [P, TILES, E])

        logits = sb("logits", [P, TILES, NE])
        row_max = sb("row_max", [P, TILES])
        shifted = sb("shifted", [P, TILES, NE])
        exped = sb("exped", [P, TILES, NE])
        row_sum = sb("row_sum", [P, TILES])
        row_inv = sb("row_inv", [P, TILES])
        scores = sb("scores", [P, TILES, NE])
        scoresT = sb("scoresT", [P, P])
        cmp = sb("cmp", [P, P])
        count = sb("count", [P, 1], BF16)
        cand = sb("cand", [P, 1], I32)
        cand_next = sb("cand_next", [P, 1], I32)
        reject = sb("reject", [P, 1], I32)
        above = sb("above", [P, P])
        equal = sb("equal", [P, P])
        gt_eq = sb("gt_eq", [P, 2])
        gt_eq16 = sb("gt_eq16", [P, 2], BF16)
        need = sb("need", [P, 1])
        eq_prior = sb("eq_prior", [P, 1])
        eq_rank = sb("eq_rank", [P, P])
        eq_kept = sb("eq_kept", [P, P])
        chosen = sb("chosen", [P, P])
        rank = sb("rank", [P, P])
        taken16 = sb("taken16", [P, 1], BF16)
        first = sb("first", [P, 1])
        last = sb("last", [P, 1])
        meta = sb("meta", [P, 3], BF16)
        past_first = sb("past_first", [P, CAP])
        in_tile = sb("in_tile", [P, CAP], BF16)
        rank_e = sb("rank_e", [P, NE, P], BF16)
        meta_e = sb("meta_e", [P, NE, 3], BF16)
        slot_meta = sb("slot_meta", [P, SLOT_TILES, NE, 3])
        slot_first = sb("slot_first", [P, SLOT_TILES, NE])
        slot_local = sb("slot_local", [P, SLOT_TILES, NE])
        before = sb("before", [P, SLOT_TILES, P], BF16)
        tok_local = sb("tok_local", [P, NE, SLOT_TILES])
        tok_index = sb("tok_index", [P, NE, SLOT_TILES], U32)

        q_aug = sb("q_aug", [P, 2, HEADS, S], BF16)
        k_aug = sb("k_aug", [P, 2, HEADS, S], BF16)
        v_aug = sb("v_aug", [P, 2, 2, HEADS, 32])
        row_m = sb("row_m", [P, 2, 2, HEADS // 2])
        m_rest = sb("m_rest", [P, 2, HEADS // 2])
        m_parts = sb("m_parts", [P, 2, 2, PARTS, HEADS // 2], BF16)
        mT = sb("mT", [PARTS * HEADS // 2, S], BF16)
        probs = sb("probs", [P, 6, 512])
        oT = sb("oT", [P, 4, S])
        o_inv = sb("o_inv", [P, HEADS])
        o_nat = sb("o_nat", [P, 2, HEADS, D])
        o_normT = sb("o_normT", [P, S])

        w1_sb = sb("w1_sb", [P, 2, HID])
        w3_sb = sb("w3_sb", [P, 2, HID])
        w2_sb = sb("w2_sb", [P, 2, HC, E])
        xg = sb("xg", [P, 2, SLOT_TILES, ROW])
        xg_scaled = sb("xg_scaled", [P, SLOT_TILES, E])
        xgT = sb("xgT", [P, CAP])
        tanh_g = sb("tanh_g", [P, CAP])
        silu2 = sb("silu2", [P, CAP])
        hid = sb("hid", [P, HC, CAP])
        y_sb = sb("y_sb", [P, 2, SLOT_TILES, E])
        sums = sb("sums", [P, TILES, E])
        result = sb("result", [P, TILES, E])

        x_in = [sem(f"x_in{c}") for c in range(CHUNKS)]
        w_in = sem("w_in")
        wp_in = sem("wp_in")
        pool_ready = sem("pool_ready")
        consts_up = sem("consts_up")
        const_ps = sem("const_ps")
        const_sb = sem("const_sb")
        neg_ones_up = sem("neg_ones_up")
        k_set = sem("k_set")
        v_set = sem("v_set")
        stats_up = sem("stats_up")
        mv_up = sem("mv_up")
        var_up = sem("var_up")
        rstd_up = sem("rstd_up")
        xn_up = sem("xn_up")
        xT_ps = sem("xT_ps")
        xT_up = sem("xT_up")
        qk_ps = sem("qk_ps")
        vg_ps = sem("vg_ps")
        bq_up = sem("bq_up")
        q_f_up = sem("q_f_up")
        k_f_up = sem("k_f_up")
        part0_up = sem("part0_up")
        rest_up = sem("rest_up")
        part1_up = sem("part1_up")
        part2_up = sem("part2_up")
        vg_up = sem("vg_up")
        parts_out = [sem(f"parts_out{c}") for c in range(CHUNKS)]
        x_bias_up = sem("x_bias_up")
        acc_out = sem("acc_out")
        gate_step = sem("gate_step")
        bits_up = sem("bits_up")
        gate_exp = sem("gate_exp")
        scores_up = sem("scores_up")
        table_out = sem("table_out")
        scT_ps = sem("scT_ps")
        search = sem("search")
        counted = sem("counted")
        count_ps = sem("count_ps")
        rejected = sem("rejected")
        next_up = sem("next_up")
        pick = sem("pick")
        gt_eq_up = sem("gt_eq_up")
        taken_up = sem("taken_up")
        rank_e_up = sem("rank_e_up")
        meta_e_up = sem("meta_e_up")
        meta_up = sem("meta_up")
        tok_counted = sem("tok_counted")
        pick_ps = sem("pick_ps")
        slots_ps = sem("slots_ps")
        tok_up = sem("tok_up")

        qk_in = [[sem(f"qk_in{b}{hp}") for hp in range(2)] for b in range(2)]
        v_up = sem("v_up")
        nat_full = sem("nat_full")
        nat_max = sem("nat_max")
        m_step = sem("m_step")
        m_in = sem("m_in")
        tr_full = sem("tr_full")
        exp_up = sem("exp_up")
        probs_up = sem("probs_up")
        last_probs_up = sem("last_probs_up")
        keep_up = sem("keep_up")
        pv_quads = sem("pv_quads")
        oT_up = sem("oT_up")
        misc_full = sem("misc_full")
        misc_free = sem("misc_free")
        post_step = sem("post_step")
        gathered = [sem("gathered0"), sem("gathered1")]
        ew_in = [sem("ew_in0"), sem("ew_in1")]
        scaled_up = sem("scaled_up")
        ff_full = sem("ff_full")
        tanh_up = sem("tanh_up")
        silu_up = sem("silu_up")
        hid_up = sem("hid_up")
        scattered = sem("scattered")
        sums_in = [sem(f"sums_in{i}") for i in range(3)]
        result_up = sem("result_up")
        stored = sem("stored")

        STEPS = 12
        BITS = TOP_BIT + 1
        LEAD = 9
        HALF_STEPS = STEPS // 2
        BITS_SETUP = 6
        BIT_STEPS = (2, 1, 2, 1, 2, 1, 2, 1, 1, 1, 1, 0)
        assert BITS_SETUP + LEAD + sum(BIT_STEPS) == BITS
        MARK, RANK, PLACE, SPREAD, SLOT_META = 11, 13, 14, 15, 16
        FIRST_EXPERT = 19
        SPACING = 8
        FIND, SCALE, TURN, GATE_UP, GATED, DOWN, SCATTER = -1, 5, 6, (7, 9), (8, 10), 11, 12

        def expert_at(n, s, stage):
            e, r = divmod(STEPS * n + s - FIRST_EXPERT - stage, SPACING)
            return e if r == 0 and 0 <= e < NE else None

        def diagonal(s):
            v = probs[:, s % 6, :]
            if s % 3 < 2:
                return v.rearrange("p (h k) -> p h k", h=2)[:, :, 0:P], 2
            return v.rearrange("p (h k) -> p h k", h=4), 4

        def maxima_at(n, s, after):
            i, r = divmod(STEPS * n + s + LEAD + 1 - after, HALF_STEPS)
            return divmod(i - 1, 2) if r == 0 and 0 < i <= 2 * B else None

        def nat_at(n, s):
            u = STEPS * n + s + LEAD
            return divmod(u, STEPS) if u < STEPS * B else None

        def bits_at(n, s):
            g = STEPS * n + s
            done = BITS_SETUP + LEAD + sum(BIT_STEPS[:g])
            return range(done, done + sum(BIT_STEPS[g:g + 1]))

        def misc_uses(n, s):
            keys = {0: [("o0", n - 1)], 4: [("o1", n - 1)], 8: [("a", n - 1)], 11: [("pr", n - 1)]}.get(s, [])
            keys = keys if n > 0 else []
            if maxima_at(n, s, 1):
                batch, half = maxima_at(n, s, 1)
                keys += [(f"m{half}", batch)]
            keys += [(x, expert_at(n, s, at)) for x, at in (("r", FIND), ("x", TURN), ("y", DOWN))
                     if expert_at(n, s, at) is not None]
            return keys

        LAST_USES = [(x, B - 1) for x in ("o0", "o1", "a", "pr")]
        MISC = {key: at for at, key in enumerate(
            [("m0", 0)] + [key for n in range(B) for s in range(STEPS) for key in misc_uses(n, s)] + LAST_USES)}

        PIECES = (slice(0, TILES // 2), slice(TILES // 2, TILES - 2), slice(TILES - 2, TILES))

        block = ctx.enter_context(nc.Block())

        @block.sync
        def _(sp):
            def load_experts(e):
                sp.dma_start(w1_sb[:, e % 2, :], w1[e]).then_inc(ew_in[e % 2], 16)
                sp.dma_start(w3_sb[:, e % 2, :], w3[e]).then_inc(ew_in[e % 2], 16)
                sp.dma_start(w2_sb[:, e % 2], w2[e].rearrange("(c p) n -> p c n", p=P)).then_inc(ew_in[e % 2], 16)

            def load_qk(n, half):
                tok = slice(n * S, (n + 1) * S)
                heads = slice(8 * half, 8 * half + 8)
                for i in range(PARTS):
                    rows = slice(i * PARTS * D, (i + 1) * PARTS * D)
                    q = qk_dram[0, i, half].rearrange("(d h) t -> d h t", d=D)[:, :, tok]
                    sp.dma_start(q_aug[rows, n % 2, heads],
                                 q.unsqueeze(0).broadcast_to([PARTS, D, 8, S])).then_inc(qk_in[n % 2][half], 16)
                    k = qk_dram[1, :, half].rearrange("j (d h) t -> j d h t", d=D)[:, :, :, tok]
                    sp.dma_start(k_aug[rows, n % 2, heads], k).then_inc(qk_in[n % 2][half], 16)

            def load_m(n, half):
                sp.wait_ge(misc_free, MISC[f"m{half}", n] + 1)
                sp.dma_start(q_aug[KS:KM, n % 2, 8 * half:8 * half + 8], mT[:]).then_inc(m_in, 16)

            for c in range(CHUNKS):
                sp.dma_start(x_nat[:, CT * c:CT * c + CT], x_tok[:, CT * c:CT * c + CT]).then_inc(x_in[c], 16)
            sp.dma_start(wqk_sb[:], w_qk).then_inc(w_in, 16)
            sp.dma_start(bqk_sb[:], b_qk).then_inc(w_in, 16)
            sp.dma_start(wvg_sb[:, 0:E], w_v).then_inc(w_in, 16)
            sp.dma_start(wvg_sb[:, E:ROW], w_gate).then_inc(w_in, 16)
            sp.dma_start(bv_sb[:], b_v.partition_broadcast(P)).then_inc(w_in, 16)
            sp.dma_start(bp_sb[:], b_p.partition_broadcast(P)).then_inc(wp_in, 16)
            sp.dma_start(wp_sb[:], w_p).then_inc(wp_in, 16)
            sp.wait_ge(neg_ones_up, 1)
            sp.dma_start(k_aug[KS:KM].rearrange("p b h t -> p (b h) t"),
                         neg_ones[:].unsqueeze(1).broadcast_to([PARTS, 2 * HEADS, S])).then_inc(k_set, 16)
            for c in range(CHUNKS):
                sp.wait_ge(part2_up, c + 1)
                for t in range(2):
                    sp.dma_start(qk_dram[t].rearrange("g a r t -> (a r) g t")[:, :, c * CHUNK:(c + 1) * CHUNK],
                                 qk_parts[:, c, t]).then_inc(parts_out[c], 16)
                if c == 0:
                    sp.wait_ge(parts_out[0], 32)
                    load_qk(0, 0)
                    load_qk(0, 1)
            load_qk(1, 0)
            load_m(0, 0)
            load_qk(1, 1)
            for c in range(1, CHUNKS):
                sp.wait_ge(parts_out[c], 32)
            sp.wait_ge(scores_up, 1)
            sp.dma_start(table.rearrange("(t p) r -> p t r", p=P), xn[:]).then_inc(table_out, 16)
            sp.wait_ge(x_bias_up, 1)
            sp.dma_start(acc.rearrange("(t p) e -> p t e", p=P), x_bias[:]).then_inc(acc_out, 16)
            load_experts(0)
            load_experts(1)

            for n in range(B):
                for s in range(STEPS):
                    if n + 2 < B and s in (5, 11):
                        sp.wait_ge(tr_full, STEPS * n + s + 1)
                        load_qk(n + 2, s // 6)
                    if maxima_at(n, s, 1):
                        load_m(*maxima_at(n, s, 1))
                    e = expert_at(n, s, DOWN)
                    if e is not None and e + 2 < NE:
                        sp.wait_ge(misc_full, MISC["y", e] + 1)
                        load_experts(e + 2)
            sp.wait_ge(scattered, 16 * SLOT_TILES * NE)
            for i, tiles in enumerate(PIECES):
                sp.dma_start(sums[:, tiles], acc.rearrange("(t p) e -> p t e", p=P)[:, tiles]).then_inc(sums_in[i], 16)
            for i, tiles in enumerate(PIECES):
                sp.wait_ge(result_up, i + 1)
                sp.dma_start(out_tok[:, tiles], result[:, tiles]).then_inc(stored, 16)
            sp.wait_ge(stored, 16 * len(PIECES))

        @block.gpsimd
        def _(pool):
            pool.memset(neg_ones[:], -1.0).then_inc(neg_ones_up, 1)
            pool.memset(ones[:], 1.0).then_inc(consts_up, 1)
            pool.memset(ones16[:], 1.0).then_inc(consts_up, 1)
            pool.memset(zero16[:], 0.0).then_inc(consts_up, 1)
            pool.memset(neg_half[:], -0.5).then_inc(consts_up, 1)
            pool.wait_ge(consts_up, 4)
            pool.affine_select(out=ident[:], in_=ones[:], compare_op=ALU.is_equal, fill=0.0, base=0,
                               pattern=[[1, P]], channel_multiplier=-1).then_inc(consts_up, 1)
            pool.affine_select(out=ident16[:], in_=ones[:], compare_op=ALU.is_equal, fill=0.0, base=0,
                               pattern=[[1, P]], channel_multiplier=-1).then_inc(consts_up, 1)
            pool.affine_select(out=exp_of_row[:].rearrange("e (t f) -> e t f", f=NE),
                               in_=ones[0:NE].rearrange("e (t f) -> e t f", f=NE),
                               compare_op=ALU.is_equal, fill=0.0, base=0,
                               pattern=[[0, TILES], [1, NE]], channel_multiplier=-1).then_inc(consts_up, 1)
            for c in range(CHUNKS):
                pool.wait_ge(mv_up, CT * (c + 1))
                pool.tensor_scalar(var_eps[:, CT * c:CT * c + CT], mean_var[:, CT * c:CT * c + CT, 1],
                                   1e-5, None, ALU.add).then_inc(var_up, 1)
                pool.wait_ge(var_up, c + 1)
                pool.tensor_tensor(rstd[:, CT * c:CT * c + CT], var_eps[:, CT * c:CT * c + CT],
                                   neg_half[:], ALU.pow).then_inc(rstd_up, 1)
            pool.affine_select(out=causal16[:], in_=zero16[:], compare_op=ALU.is_ge, fill=MASKED, base=0,
                               pattern=[[0, 4], [-1, P]], channel_multiplier=1).then_inc(consts_up, 1)
            pool.memset(keep[:], 2.0).then_inc(keep_up, 1)
            pool.wait_ge(keep_up, 1)
            pool.affine_select(out=keep[:], in_=keep[:], compare_op=ALU.is_ge, fill=0.0, base=0,
                               pattern=[[1, P]], channel_multiplier=-1).then_inc(keep_up, 1)
            pool.iota(exponents[:], pattern=[[-1, BITS]], base=127 + TOP_BIT,
                      channel_multiplier=0).then_inc(consts_up, 1)
            pool.memset(v_aug[:], 0.0).then_inc(v_set, 1)
            pool.wait_ge(v_set, 1)
            pool.memset(v_aug[:, :, :, :, D:D + 1], 1.0).then_inc(v_set, 1)

            def last_part(c):
                pool.wait_ge(part1_up, c + 1)
                pool.tensor_tensor(qk_parts[:, c, :, 2], qk_rest[:, c % 2], qk_parts[:, c, :, 1],
                                   ALU.subtract).then_inc(part2_up, 1)

            for c in range(CHUNKS):
                last_part(c)
            pool.iota(slot_row[:], pattern=[[1, CAP]], base=0, channel_multiplier=0,
                      allow_small_or_imprecise_dtypes=True).then_inc(consts_up, 1)
            pool.iota(slot_col[:], pattern=[[P, SLOT_TILES]], base=0, channel_multiplier=1,
                      allow_small_or_imprecise_dtypes=True).then_inc(consts_up, 1)
            pool.wait_ge(const_sb, 2)
            pool.affine_select(out=prior16[:], in_=same16[:], compare_op=ALU.is_gt, fill=0.0, base=0,
                               pattern=[[1, P]], channel_multiplier=-1).then_inc(pool_ready, 1)
            pool.wait_ge(wp_in, 32)
            for c in range(CHUNKS):
                pool.wait_ge(x_in[c], 16)
            pool.tensor_tensor(x_bias[:], x_nat[:], bp_sb[:].unsqueeze(1).broadcast_to([P, TILES, E]),
                               ALU.add).then_inc(x_bias_up, 1)

            def gather(e, s):
                if s == 0:
                    pool.wait_ge(tok_up, e + 1)
                    pool.wait_ge(table_out, 16)
                    if e >= 2:
                        pool.wait_ge(scaled_up, e - 1)
                pool.indirect_dma_start(
                    out=xg[:, e % 2, s, :], out_offset=None, in_=table[:, :],
                    in_offset=bass.IndirectOffsetOnAxis(ap=tok_index[:, e, s:s + 1], axis=0)
                ).then_inc(gathered[e % 2], 16)

            def scatter(e, s):
                if s == 0:
                    pool.wait_ge(misc_free, MISC["y", e] + 1)
                    pool.wait_ge(acc_out, 16)
                    if e > 0:
                        pool.wait_ge(scattered, 16 * SLOT_TILES * e)
                pool.indirect_dma_start(
                    out=acc[:, :], out_offset=bass.IndirectOffsetOnAxis(ap=tok_index[:, e, s:s + 1], axis=0),
                    in_=y_sb[:, e % 2, s, :], in_offset=None, compute_op=ALU.add
                ).then_inc(scattered, 16)

            def mask_unit(n, s):
                pool.wait_ge(exp_up, STEPS * n + s + 1)
                v, heads = diagonal(s)
                pool.affine_select(out=v, in_=v, compare_op=ALU.is_ge, fill=0.0, base=0,
                                   pattern=[[0, heads], [1, P]], channel_multiplier=-1).then_inc(probs_up, 1)

            for n in range(B):
                for s in range(STEPS):
                    if STEPS * n + s == RANK + 1:
                        pool.wait_ge(taken_up, 1)
                        pool.tensor_tensor(rank_e[:], rank[:].unsqueeze(1).broadcast_to([P, NE, P]),
                                           sel_exp[:].unsqueeze(2).broadcast_to([P, NE, P]),
                                           ALU.mult).then_inc(rank_e_up, 1)
                    if n < B - 1:
                        mask_unit(n, s)
                    for tile in range(SLOT_TILES):
                        if expert_at(n, s, tile) is not None:
                            gather(expert_at(n, s, tile), tile)
                        if expert_at(n, s, SCATTER + tile) is not None:
                            scatter(expert_at(n, s, SCATTER + tile), tile)

        @block.scalar
        def _(act):
            def take_xT(c):
                act.wait_ge(xT_ps, c + 1)
                act.activation(xnT[:, c * CHUNK:(c + 1) * CHUNK], nat_ps[c % 2][:], ACT.Copy).then_inc(xT_up, 1)

            def take_qk(c):
                act.wait_ge(qk_ps, 2 * c + 1)
                if c == 0:
                    act.wait_ge(w_in, 80)
                    act.wait_ge(bq_up, 1)
                if c >= 2:
                    act.wait_ge(rest_up, c - 1)
                act.activation(qk_f[:, c % 2, 0], tr_ps[0][:], ACT.Identity, bias=bq_scaled[:],
                               scale=INV_SQRT_D).then_inc(q_f_up, 1)
                act.wait_ge(qk_ps, 2 * c + 2)
                act.activation(qk_f[:, c % 2, 1], tr_ps[1][:], ACT.Identity, bias=bqk_sb[:, 1:2]).then_inc(k_f_up, 1)

            def first_part(c):
                act.wait_ge(k_f_up, c + 1)
                act.wait_ge(q_f_up, c + 1)
                act.activation(qk_parts[:, c, :, 0], qk_f[:, c % 2], ACT.Copy).then_inc(part0_up, 1)

            def second_part(c):
                act.wait_ge(rest_up, c + 1)
                act.activation(qk_parts[:, c, :, 1], qk_rest[:, c % 2], ACT.Copy).then_inc(part1_up, 1)

            take_xT(0)
            take_xT(1)
            take_qk(0)
            first_part(0)
            take_xT(2)
            take_xT(3)
            second_part(0)
            act.wait_ge(gate_step, 2)
            act.activation(exped[:], shifted[:], ACT.Exp).then_inc(gate_exp, 1)
            take_qk(1)
            for c in range(1, CHUNKS):
                first_part(c)
                if c + 1 < CHUNKS:
                    take_qk(c + 1)
                second_part(c)

            def copy_v(n):
                act.activation(v_aug[:, n % 2, :, :, 0:D],
                               v_nat[:, 2 * n:2 * n + 2, :].rearrange("p u (h d) -> p u h d", d=D),
                               ACT.Copy).then_inc(v_up, 1)

            act.wait_ge(vg_up, TILES)
            act.wait_ge(v_set, 2)
            copy_v(0)

            def take(key, out, in_):
                act.wait_ge(misc_full, MISC[key] + 1)
                act.activation(out, in_, ACT.Copy).then_inc(misc_free, 1)

            def take_misc(key):
                what, i = key
                if what in ("m0", "m1"):
                    half = int(what[1])
                    if i > 0 or half > 0:
                        act.wait_ge(m_in, 16 * (2 * i + half))
                    take(key, mT[:], misc_ps[:].bitcast(BF16)[0:PARTS * HEADS // 2, 0:S])
                elif what == "a":
                    take(key, o_normT[:], misc_ps[:, 0:S])
                elif what == "pr":
                    take(key, result[:, 2 * i:2 * i + 2, :], misc_ps[:, 0:S].rearrange("p (u e) -> p u e", u=2))
                elif what == "x":
                    take(key, xgT[:], misc_ps[:])
                elif what == "y":
                    if i >= 2:
                        act.wait_ge(scattered, 16 * SLOT_TILES * (i - 1))
                    take(key, y_sb[:, i % 2], misc_ps[:].rearrange("p (s n) -> p s n", s=SLOT_TILES))

            def exp_unit(n, s):
                act.wait_ge(tr_full, STEPS * n + s + 1)
                if s % 3 == 0 and (n > 0 or s >= 6):
                    act.wait_ge(pv_quads, 4 * n + s // 3 - 1)
                act.activation(probs[:, s % 6, :], tr_ps[s % 2][:], ACT.Exp).then_inc(exp_up, 1)

            def take_o(n, half):
                act.wait_ge(pv_quads, 4 * n + 2 * half + 2)
                if n > 0:
                    act.wait_ge(misc_full, MISC[f"o{half}", n - 1] + 1)
                act.activation(oT[:, 2 * half:2 * half + 2, :], pv_ps[:].rearrange("p (q t) -> p q t", q=2),
                               ACT.Copy).then_inc(oT_up, 1)

            def tanh(e, c):
                act.wait_ge(ff_full, 4 * e + 2 * c + 1)
                if e > 0 or c > 0:
                    act.wait_ge(silu_up, 2 * e + c)
                act.activation(tanh_g[:], ff_ps[0][:], ACT.Tanh, scale=0.5).then_inc(tanh_up, 1)

            take_misc(("m0", 0))
            for n in range(B):
                for s in range(STEPS):
                    exp_unit(n, s)
                    if s == 2 and n > 0:
                        take_o(n - 1, 1)
                    if s == 8:
                        take_o(n, 0)
                    for key in misc_uses(n, s):
                        take_misc(key)
                    for c in range(HC):
                        if expert_at(n, s, GATE_UP[c]) is not None:
                            tanh(expert_at(n, s, GATE_UP[c]), c)
                    if s == 9 and n < B - 1:
                        if n > 0:
                            act.wait_ge(pv_quads, 4 * n)
                        copy_v(n + 1)
            take_o(B - 1, 1)
            take_misc(("a", B - 1))

        @block.vector
        def _(dve):
            def find_stats(c):
                dve.wait_ge(x_in[c], 16)
                for t in range(CT * c, CT * c + CT):
                    dve.bn_stats(stats[:, t, :], x_nat[:, t, :]).then_inc(stats_up, 1)
                for t in range(CT * c, CT * c + CT):
                    dve.wait_ge(stats_up, t + 1)
                    dve.bn_aggr(mean_var[:, t, :], stats[:, t, :]).then_inc(mv_up, 1)

            def normalize(c):
                dve.wait_ge(rstd_up, c + 1)
                for t in range(CT * c, CT * c + CT):
                    dve.tensor_scalar(xn[:, t, 0:E], x_nat[:, t, :], mean_var[:, t, 0:1], rstd[:, t:t + 1],
                                      ALU.subtract, ALU.mult).then_inc(xn_up, 1)

            def rest(c):
                dve.wait_ge(part0_up, c + 1)
                if c >= 2:
                    dve.wait_ge(part2_up, c - 1)
                dve.tensor_tensor(qk_rest[:, c % 2], qk_f[:, c % 2], qk_parts[:, c, :, 0],
                                  ALU.subtract).then_inc(rest_up, 1)

            def take_vg(c):
                for u in range(2):
                    dve.wait_ge(vg_ps, 2 * c + u + 1)
                    t = CT * c + 2 * u
                    ps = ff_ps[u][:, 0:2 * ROW].rearrange("p (t r) -> p t r", t=2)
                    dve.tensor_tensor(v_nat[:, t:t + 2, :], ps[:, :, 0:E],
                                      bv_sb[:].unsqueeze(1).broadcast_to([P, 2, E]), ALU.add).then_inc(vg_up, 1)
                    dve.tensor_copy(logits[:, t:t + 2, :], ps[:, :, E:ROW]).then_inc(vg_up, 1)

            find_stats(0)
            for c in range(CHUNKS):
                if c + 1 < CHUNKS:
                    find_stats(c + 1)
                normalize(c)
            dve.wait_ge(const_ps, 1)
            dve.tensor_copy(same16[:], misc_ps[:, 0:P]).then_inc(const_sb, 1)
            dve.tensor_copy(sel_exp[:], misc_ps[:, P:P + NE]).then_inc(const_sb, 1)

            def make_bits():
                dve.wait_ge(consts_up, 9)
                dve.tensor_scalar(bits_f[:].bitcast(I32), exponents[:], 23, None,
                                  ALU.logical_shift_left).then_inc(bits_up, 1)
                dve.memset(cand[:], CAND_START).then_inc(bits_up, 1)
                dve.wait_ge(bits_up, 2)
                dve.tensor_copy(bits_i[:], bits_f[:]).then_inc(bits_up, 1)

            def spread(a):
                return a[:].unsqueeze(2).broadcast_to([P, TILES, NE])

            def shift_logits():
                dve.wait_ge(vg_up, TILES)
                dve.tensor_reduce(row_max[:], logits[:], AX_X, ALU.max).then_inc(gate_step, 1)
                dve.wait_ge(gate_step, 1)
                dve.tensor_tensor(shifted[:], logits[:], spread(row_max), ALU.subtract).then_inc(gate_step, 1)

            def make_scores():
                dve.wait_ge(gate_exp, 1)
                dve.tensor_reduce(row_sum[:], exped[:], AX_X, ALU.add).then_inc(gate_step, 1)
                dve.wait_ge(gate_step, 3)
                dve.reciprocal(row_inv[:], row_sum[:]).then_inc(gate_step, 1)
                dve.wait_ge(gate_step, 4)
                dve.tensor_tensor(scores[:], exped[:], spread(row_inv), ALU.mult).then_inc(gate_step, 1)
                dve.wait_ge(gate_step, 5)
                dve.tensor_copy(xn[:, :, E:ROW], scores[:]).then_inc(scores_up, 1)

            def try_bit(k):
                dve.wait_ge(search, k + 1)
                dve.tensor_scalar(cmp[:], scoresT[:], cand[:].bitcast(F32), 0.0, ALU.is_ge, ALU.add,
                                  accum_out=count[:]).then_inc(counted, 1)
                if k + 1 < BITS:
                    dve.tensor_tensor(cand_next[:], cand[:], bits_i[:, k + 1:k + 2],
                                      ALU.bitwise_or).then_inc(next_up, 1)

            def settle_bit(k):
                dve.wait_ge(count_ps, k + 1)
                dve.scalar_tensor_tensor(out=reject[:], in0=ff_ps[1][:, 0:1], scalar=CAP - 0.5,
                                         in1=bits_f[:, k:k + 1], op0=ALU.is_lt, op1=ALU.mult).then_inc(rejected, 1)
                dve.wait_ge(rejected, k + 1)
                if k + 1 < BITS:
                    dve.wait_ge(next_up, k + 1)
                    base = cand_next
                else:
                    base = cand
                dve.tensor_tensor(cand[:], base[:], reject[:], ALU.bitwise_xor).then_inc(search, 1)

            def search_step(k):
                if k > 0:
                    settle_bit(k - 1)
                try_bit(k)

            dve.wait_ge(w_in, 80)
            dve.tensor_scalar(bq_scaled[:], bqk_sb[:, 0:1], INV_SQRT_D, None, ALU.mult).then_inc(bq_up, 1)
            take_vg(0)
            make_bits()
            take_vg(1)
            rest(0)
            take_vg(2)
            take_vg(3)
            shift_logits()
            make_scores()
            dve.wait_ge(scT_ps, 1)
            dve.tensor_copy(scoresT[:], misc_ps[:, 0:P]).then_inc(search, 1)
            dve.wait_ge(bits_up, 3)
            search_step(0)
            rest(1)
            search_step(1)
            search_step(2)
            search_step(3)
            rest(2)
            search_step(4)
            search_step(5)

            picks = [0]

            def link(ins):
                picks[0] += 1
                ins.then_inc(pick, 1)
                dve.wait_ge(pick, picks[0])

            def mark_tokens():
                settle_bit(BITS - 1)
                dve.wait_ge(search, BITS + 1)
                limit = cand[:].bitcast(F32)
                link(dve.tensor_scalar(above[:], scoresT[:], limit, 0.0, ALU.is_gt, ALU.add,
                                       accum_out=gt_eq[:, 0:1]))
                link(dve.tensor_scalar(equal[:], scoresT[:], limit, 0.0, ALU.is_equal, ALU.add,
                                       accum_out=gt_eq[:, 1:2]))
                dve.tensor_copy(gt_eq16[:], gt_eq[:]).then_inc(gt_eq_up, 1)

            def rank_tokens():
                dve.wait_ge(pick_ps, 1)
                link(dve.tensor_scalar(need[:], ff_ps[1][:, 0:1], -1.0, float(CAP), ALU.mult, ALU.add))
                link(dve.tensor_copy(eq_prior[:], ff_ps[1][:, 1:2]))
                link(dve.tensor_tensor_scan(eq_rank[:], ones[:], equal[:], eq_prior[:], ALU.mult, ALU.add))
                link(dve.scalar_tensor_tensor(out=eq_kept[:], in0=eq_rank[:], scalar=need[:], in1=equal[:],
                                              op0=ALU.is_le, op1=ALU.mult))
                link(dve.tensor_tensor(chosen[:], above[:], eq_kept[:], ALU.add))
                link(dve.tensor_tensor_scan(rank[:], ones[:], chosen[:], 0.0, ALU.mult, ALU.add))
                dve.tensor_copy(taken16[:], rank[:, P - 1:P]).then_inc(taken_up, 1)

            def place_rows():
                dve.wait_ge(pick_ps, 2)
                dve.wait_ge(consts_up, 11)
                link(dve.tensor_copy(first[:], ff_ps[1][:, 0:1]))
                link(dve.tensor_copy(meta[:, 0:1], ff_ps[1][:, 1:2]))
                link(dve.tensor_tensor(last[:], first[:], rank[:, P - 1:P], ALU.add))
                link(dve.tensor_copy(meta[:, 1:2], first[:]))
                link(dve.tensor_tensor(meta[:, 2:3], first[:], meta[:, 1:2], ALU.subtract))
                link(dve.tensor_scalar(past_first[:], slot_row[:], first[:], None, ALU.is_ge))

            def spread_rows():
                link(dve.scalar_tensor_tensor(out=in_tile[:], in0=slot_row[:], scalar=last[:], in1=past_first[:],
                                              op0=ALU.is_lt, op1=ALU.mult))
                dve.tensor_tensor(meta_e[:], meta[:].unsqueeze(1).broadcast_to([P, NE, 3]),
                                  sel_exp[:].unsqueeze(2).broadcast_to([P, NE, 3]), ALU.mult).then_inc(meta_e_up, 1)

            def take_meta():
                dve.wait_ge(slots_ps, 1)
                dve.tensor_copy(slot_meta[:], ff_ps[0][:, 0:SLOT_TILES * NE * 3].rearrange(
                    "p (s e m) -> p s e m", s=SLOT_TILES, e=NE)).then_inc(meta_up, 1)
                dve.wait_ge(meta_up, 1)
                link(dve.tensor_tensor(slot_first[:], slot_meta[:, :, :, 1], slot_meta[:, :, :, 2], ALU.add))
                link(dve.tensor_tensor(slot_local[:], slot_col[:].unsqueeze(2).broadcast_to([P, SLOT_TILES, NE]),
                                       slot_first[:], ALU.subtract))

            def find_tokens(e):
                dve.wait_ge(misc_full, MISC["r", e] + 1)
                dve.tensor_tensor(before[:], misc_ps[:].rearrange("p (s t) -> p s t", s=SLOT_TILES),
                                  slot_local[:, :, e:e + 1].broadcast_to([P, SLOT_TILES, P]),
                                  ALU.is_le).then_inc(misc_free, 1)
                dve.wait_ge(misc_free, MISC["r", e] + 1)
                dve.tensor_reduce(tok_local[:, e, :], before[:], AX_X, ALU.add).then_inc(tok_counted, 1)
                dve.wait_ge(tok_counted, e + 1)
                dve.scalar_tensor_tensor(out=tok_index[:, e, :], in0=slot_meta[:, :, e, 0], scalar=float(P),
                                         in1=tok_local[:, e, :], op0=ALU.mult, op1=ALU.add).then_inc(tok_up, 1)

            def max_unit(n, v):
                q, j = v // 3, v % 3
                dve.wait_ge(nat_full, STEPS * n + v + 1)
                if j == 0:
                    dst, heads = row_m[:, q // 2, 0, 4 * (q % 2):4 * (q % 2) + 4], 4
                else:
                    h = 4 * (q % 2) + 2 * (j - 1)
                    dst, heads = row_m[:, q // 2, 1, h:h + 2], 2
                dve.tensor_reduce(dst, nat_ps[v % 2][:].rearrange("p (h k) -> p h k", h=heads),
                                  AX_X, ALU.max).then_inc(nat_max, 1)

            def split_m(n, half):
                m, parts, done = row_m[:, half], m_parts[:, half], 4 * (2 * n + half)
                dve.wait_ge(nat_max, STEPS * n + HALF_STEPS * (half + 1))
                dve.tensor_copy(parts[:, :, 0, :], m).then_inc(m_step, 1)
                dve.wait_ge(m_step, done + 1)
                dve.tensor_tensor(m_rest[:], m, parts[:, :, 0, :], ALU.subtract).then_inc(m_step, 1)
                dve.wait_ge(m_step, done + 2)
                dve.tensor_copy(parts[:, :, 1, :], m_rest[:]).then_inc(m_step, 1)
                dve.wait_ge(m_step, done + 3)
                dve.tensor_tensor(parts[:, :, 2, :], m_rest[:], parts[:, :, 1, :],
                                  ALU.subtract).then_inc(m_step, 1)

            for v in range(LEAD):
                search_step(BITS_SETUP + v)
                if v == 1:
                    rest(3)
                max_unit(0, v)
                if v == HALF_STEPS - 1:
                    split_m(0, 0)

            def scale_rows(e):
                dve.wait_ge(gathered[e % 2], 16 * SLOT_TILES * (e // 2 + 1))
                if e > 0:
                    dve.wait_ge(misc_full, MISC["x", e - 1] + 1)
                dve.tensor_tensor(xg_scaled[:], xg[:, e % 2, :, 0:E],
                                  xg[:, e % 2, :, E + e:E + e + 1].broadcast_to([P, SLOT_TILES, E]),
                                  ALU.mult).then_inc(scaled_up, 1)

            def take_o(n, half):
                o = misc_ps[:].rearrange("p (h r) -> p h r", r=32)
                dve.wait_ge(misc_full, MISC[f"o{half}", n] + 1)
                dve.reciprocal(o_inv[:], o[:, :, D]).then_inc(post_step, 1)
                dve.wait_ge(post_step, 2 * n + half + 1)
                dve.tensor_tensor(o_nat[:, :, 8 * half:8 * half + 8, :],
                                  o[:, :, 0:D].rearrange("p (u h) d -> p u h d", u=2),
                                  o_inv[:].rearrange("p (u h) -> p u h", u=2).unsqueeze(3).broadcast_to([P, 2, 8, D]),
                                  ALU.mult).then_inc(misc_free, 1)

            def gated(e, c):
                dve.wait_ge(tanh_up, 2 * e + c + 1)
                dve.scalar_tensor_tensor(out=silu2[:], in0=tanh_g[:], scalar=1.0, in1=ff_ps[0][:],
                                         op0=ALU.add, op1=ALU.mult).then_inc(silu_up, 1)
                dve.wait_ge(silu_up, 2 * e + c + 1)
                dve.wait_ge(ff_full, 4 * e + 2 * c + 2)
                dve.scalar_tensor_tensor(out=hid[:, c, :], in0=silu2[:], scalar=0.5, in1=ff_ps[1][:],
                                         op0=ALU.mult, op1=ALU.mult).then_inc(hid_up, 1)

            def mask_last(s):
                dve.wait_ge(exp_up, STEPS * (B - 1) + s + 1)
                if s == 0:
                    dve.wait_ge(keep_up, 2)
                v, heads = diagonal(s)
                dve.tensor_tensor(v, v, keep[:].unsqueeze(1).broadcast_to([P, heads, P]),
                                  ALU.min).then_inc(last_probs_up, 1)

            for n in range(B):
                for s in range(STEPS):
                    for c in range(HC):
                        if expert_at(n, s, GATED[c]) is not None:
                            gated(expert_at(n, s, GATED[c]), c)
                    for k in bits_at(n, s)[:1]:
                        search_step(k)
                    if nat_at(n, s):
                        max_unit(*nat_at(n, s))
                    for k in bits_at(n, s)[1:]:
                        search_step(k)
                    if maxima_at(n, s, 0):
                        split_m(*maxima_at(n, s, 0))
                    if expert_at(n, s, SCALE) is not None:
                        scale_rows(expert_at(n, s, SCALE))
                    if s in (0, 4) and n > 0:
                        take_o(n - 1, int(s == 4))
                    if n == B - 1:
                        mask_last(s)
                    g = STEPS * n + s
                    if g == MARK:
                        mark_tokens()
                    if g == RANK:
                        rank_tokens()
                    if g == PLACE:
                        place_rows()
                    if g == SPREAD:
                        spread_rows()
                    if g == SLOT_META:
                        take_meta()
                    if expert_at(n, s, FIND) is not None:
                        find_tokens(expert_at(n, s, FIND))
            take_o(B - 1, 0)
            take_o(B - 1, 1)
            for i in range(2):
                dve.wait_ge(sums_in[i], 16)
                dve.wait_ge(misc_free, MISC["pr", PIECES[i].stop // 2 - 1] + 1)
                dve.tensor_tensor(result[:, PIECES[i]], result[:, PIECES[i]], sums[:, PIECES[i]],
                                  ALU.add).then_inc(result_up, 1)
            dve.wait_ge(sums_in[2], 16)
            dve.wait_ge(misc_full, MISC["pr", B - 1] + 1)
            dve.tensor_tensor(result[:, PIECES[2]], misc_ps[:, 0:S].rearrange("p (u e) -> p u e", u=2),
                              sums[:, PIECES[2]], ALU.add).then_inc(result_up, 1)

        @block.tensor
        def _(pe):
            pe.wait_ge(consts_up, 7)
            pe.matmul(misc_ps[:, 0:P], exp_of_row[:], exp_of_row[:], start=True, stop=True)
            pe.matmul(misc_ps[:, P:P + NE], exp_of_row[:], ident16[0:NE, 0:NE], start=True,
                      stop=True).then_inc(const_ps, 1)

            def turn_x(c):
                pe.wait_ge(xn_up, CT * c + CT)
                if c >= 2:
                    pe.wait_ge(xT_up, c - 1)
                for u in range(CT):
                    ins = pe.transpose(nat_ps[c % 2][:, u * P:(u + 1) * P], xn[:, CT * c + u, 0:E], ident[:])
                ins.then_inc(xT_ps, 1)

            def project_qk(c):
                pe.wait_ge(xT_up, c + 1)
                if c == 0:
                    pe.wait_ge(w_in, 80)
                else:
                    pe.wait_ge(q_f_up, c)
                    pe.wait_ge(k_f_up, c)
                for t in range(2):
                    pe.matmul(tr_ps[t][:], wqk_sb[:, t, :], xnT[:, c * CHUNK:(c + 1) * CHUNK],
                              start=True, stop=True).then_inc(qk_ps, 1)

            def project_vg(c):
                pe.wait_ge(xT_up, c + 1)
                if c == 0:
                    pe.wait_ge(w_in, 80)
                else:
                    pe.wait_ge(vg_up, CT * c)
                for u in range(2):
                    for v in range(2):
                        t = CT * c + 2 * u + v
                        ins = pe.matmul(ff_ps[u][:, v * ROW:(v + 1) * ROW], xnT[:, t * P:(t + 1) * P], wvg_sb[:],
                                        start=True, stop=True)
                    ins.then_inc(vg_ps, 1)

            def count_bit(k):
                pe.wait_ge(counted, k + 1)
                pe.matmul(ff_ps[1][:, 0:1], same16[:], count[:], start=True, stop=True).then_inc(count_ps, 1)

            turn_x(0)
            turn_x(1)
            project_vg(0)
            project_qk(0)
            turn_x(2)
            project_vg(1)
            turn_x(3)
            project_vg(2)
            project_vg(3)
            project_qk(1)
            pe.wait_ge(const_sb, 2)
            pe.wait_ge(scores_up, 1)
            pe.transpose(misc_ps[:, 0:P], scores[:].rearrange("p t e -> p (t e)"), ident[:]).then_inc(scT_ps, 1)
            count_bit(0)
            project_qk(2)
            count_bit(1)
            count_bit(2)
            project_qk(3)
            count_bit(3)
            count_bit(4)
            count_bit(5)

            def count_marked():
                pe.wait_ge(gt_eq_up, 1)
                pe.wait_ge(pool_ready, 1)
                pe.matmul(ff_ps[1][:, 0:1], same16[:], gt_eq16[:, 0:1], start=True, stop=True)
                pe.matmul(ff_ps[1][:, 1:2], prior16[:], gt_eq16[:, 1:2], start=True, stop=True).then_inc(pick_ps, 1)

            def count_taken():
                pe.wait_ge(taken_up, 1)
                pe.matmul(ff_ps[1][:, 0:1], prior16[:], taken16[:], start=True, stop=True)
                pe.matmul(ff_ps[1][:, 1:2], prior16[:], ones16[:], start=True, stop=True).then_inc(pick_ps, 1)

            def slot_rows():
                pe.wait_ge(meta_e_up, 1)
                for s in range(SLOT_TILES):
                    ins = pe.matmul(ff_ps[0][:, s * NE * 3:(s + 1) * NE * 3], in_tile[:, s * P:(s + 1) * P],
                                    meta_e[:].rearrange("p e m -> p (e m)"), start=True, stop=True)
                ins.then_inc(slots_ps, 1)

            def slot_ranks(e):
                if e == 0:
                    pe.wait_ge(rank_e_up, 1)
                use(("r", e))
                for s in range(SLOT_TILES):
                    ins = pe.matmul(misc_ps[:, s * P:(s + 1) * P], in_tile[:, s * P:(s + 1) * P],
                                    rank_e[:, e, :], start=True, stop=True)
                ins.then_inc(misc_full, 1)

            def nat_unit(n, v):
                q, j = v // 3, v % 3
                p = n % 2
                ps = nat_ps[v % 2]
                if v in (0, 6):
                    pe.wait_ge(qk_in[p][q // 2], 96 * (n // 2 + 1))
                if n > 0 or v >= 2:
                    pe.wait_ge(nat_max, STEPS * n + v - 1)
                if j == 0:
                    pe.matmul(ps[:], ident16[:], causal16[:].rearrange("p a k -> p (a k)"), start=True, stop=False,
                              skip_group_check=True)
                    for c in range(4):
                        h = 4 * q + c
                        ins = pe.matmul(ps[:, c * P:(c + 1) * P], q_aug[0:KS, p, h, 0:P], k_aug[0:KS, p, h, 0:P],
                                        start=False, stop=True, skip_group_check=True)
                else:
                    pe.matmul(ps[:].rearrange("p (h k) -> p h k", h=2)[:, :, P:S], ident16[:], causal16[:, 0:2, :],
                              start=True, stop=False, skip_group_check=True)
                    for c in range(2):
                        h = 4 * q + 2 * (j - 1) + c
                        ins = pe.matmul(ps[:, c * S:(c + 1) * S], q_aug[0:KS, p, h, P:S], k_aug[0:KS, p, h, 0:S],
                                        start=False, stop=True, skip_group_check=True)
                ins.then_inc(nat_full, 1)

            def tr_unit(n, s):
                q, j = s // 3, s % 3
                p = n % 2
                ps = tr_ps[s % 2]
                if s % HALF_STEPS == 0:
                    pe.wait_ge(m_in, 16 * (2 * n + s // HALF_STEPS + 1))
                if n == 0 and s == 0:
                    pe.wait_ge(k_set, 16)
                if n > 0 or s >= 2:
                    pe.wait_ge(exp_up, STEPS * n + s - 1)
                if j < 2:
                    for c in range(2):
                        h = 4 * q + 2 * j + c
                        ins = pe.matmul(ps[:, c * S:(c + 1) * S], k_aug[0:KM, p, h, 0:P], q_aug[0:KM, p, h, :],
                                        start=True, stop=True)
                else:
                    for c in range(4):
                        h = 4 * q + c
                        ins = pe.matmul(ps[:, c * P:(c + 1) * P], k_aug[0:KM, p, h, P:S], q_aug[0:KM, p, h, P:S],
                                        start=True, stop=True)
                ins.then_inc(tr_full, 1)

            def pv(n, q):
                if n < B - 1:
                    pe.wait_ge(probs_up, STEPS * n + 3 * q + 3)
                else:
                    pe.wait_ge(last_probs_up, 3 * q + 3)
                if q == 0:
                    pe.wait_ge(v_up, n + 1)
                if q % 2 == 0 and (n > 0 or q > 0):
                    pe.wait_ge(oT_up, 2 * n + q // 2)
                col = (q % 2) * S
                for c in range(4):
                    pe.matmul(pv_ps[32 * c:32 * c + 32, col:col + S], v_aug[:, n % 2, 0, 4 * q + c, :],
                              probs[:, (3 * q + c // 2) % 6, (c % 2) * S:(c % 2) * S + S], start=True, stop=False,
                              tile_position=(0, 32 * c), skip_group_check=True)
                for c in range(4):
                    ins = pe.matmul(pv_ps[32 * c:32 * c + 32, col + P:col + S], v_aug[:, n % 2, 1, 4 * q + c, :],
                                    probs[:, (3 * q + 2) % 6, c * P:(c + 1) * P], start=False, stop=True,
                                    tile_position=(0, 32 * c), skip_group_check=True)
                ins.then_inc(pv_quads, 1)

            def use(key):
                if MISC[key] > 0:
                    pe.wait_ge(misc_free, MISC[key])

            def turn_m(n, half):
                pe.wait_ge(m_step, 4 * (2 * n + half + 1))
                use((f"m{half}", n))
                for u in range(2):
                    ins = pe.transpose(misc_ps[:].bitcast(BF16)[0:PARTS * HEADS // 2, u * P:(u + 1) * P],
                                       m_parts[:, half, u].rearrange("p s h -> p (s h)"), ident16[:])
                ins.then_inc(misc_full, 1)

            def turn_rows(e):
                pe.wait_ge(scaled_up, e + 1)
                use(("x", e))
                for s in range(SLOT_TILES):
                    ins = pe.transpose(misc_ps[:, s * P:(s + 1) * P], xg_scaled[:, s, :], ident[:])
                ins.then_inc(misc_full, 1)

            def gate_up(e, c):
                if c == 0:
                    pe.wait_ge(misc_free, MISC["x", e] + 1)
                    pe.wait_ge(ew_in[e % 2], 48 * (e // 2 + 1))
                if e > 0 or c > 0:
                    pe.wait_ge(hid_up, 2 * e + c)
                pe.matmul(ff_ps[0][:], w1_sb[:, e % 2, c * P:(c + 1) * P], xgT[:], start=True, stop=True
                          ).then_inc(ff_full, 1)
                pe.matmul(ff_ps[1][:], w3_sb[:, e % 2, c * P:(c + 1) * P], xgT[:], start=True, stop=True
                          ).then_inc(ff_full, 1)

            def down(e):
                pe.wait_ge(hid_up, 2 * e + 2)
                use(("y", e))
                for s in range(SLOT_TILES):
                    for c in range(HC):
                        ins = pe.matmul(misc_ps[:, s * P:(s + 1) * P], hid[:, c, s * P:(s + 1) * P],
                                        w2_sb[:, e % 2, c, :], start=(c == 0), stop=(c == HC - 1))
                ins.then_inc(misc_full, 1)

            def turn_o(n, half):
                pe.wait_ge(oT_up, 2 * n + half + 1)
                use((f"o{half}", n))
                for u in range(2):
                    for q in range(2):
                        ins = pe.transpose(misc_ps[:, (2 * u + q) * P:(2 * u + q + 1) * P],
                                           oT[:, 2 * half + q, u * P:(u + 1) * P], ident[:])
                ins.then_inc(misc_full, 1)

            def turn_a(n):
                use(("a", n))
                for u in range(2):
                    ins = pe.transpose(misc_ps[:, u * P:(u + 1) * P], o_nat[:, u].rearrange("p h d -> p (h d)"),
                                       ident[:])
                ins.then_inc(misc_full, 1)

            def project(n):
                use(("pr", n))
                for u in range(2):
                    ins = pe.matmul(misc_ps[:, u * E:(u + 1) * E], o_normT[:, u * P:(u + 1) * P], wp_sb[:],
                                    start=True, stop=True)
                ins.then_inc(misc_full, 1)

            def fill_misc(key):
                what, i = key
                if what in ("o0", "o1"):
                    turn_o(i, int(what[1]))
                elif what == "a":
                    turn_a(i)
                elif what == "pr":
                    project(i)
                elif what in ("m0", "m1"):
                    turn_m(i, int(what[1]))
                elif what == "r":
                    slot_ranks(i)
                elif what == "x":
                    turn_rows(i)
                else:
                    down(i)

            pe.wait_ge(consts_up, 8)
            pe.wait_ge(wp_in, 32)
            pe.wait_ge(search, 1)
            for v in range(LEAD):
                nat_unit(0, v)
                count_bit(BITS_SETUP + v)
                if v == HALF_STEPS:
                    turn_m(0, 0)

            for n in range(B):
                for s in range(STEPS):
                    if nat_at(n, s):
                        nat_unit(*nat_at(n, s))
                    tr_unit(n, s)
                    for k in bits_at(n, s)[:1]:
                        count_bit(k)
                    if s == 1 and n > 0:
                        pv(n - 1, 3)
                    if s in (4, 7, 10):
                        pv(n, s // 3 - 1)
                    for k in bits_at(n, s)[1:]:
                        count_bit(k)
                    for key in misc_uses(n, s):
                        fill_misc(key)
                    for c in range(HC):
                        if expert_at(n, s, GATE_UP[c]) is not None:
                            gate_up(expert_at(n, s, GATE_UP[c]), c)
                    g = STEPS * n + s
                    if g == MARK + 1:
                        count_marked()
                    if g == RANK + 1:
                        count_taken()
                    if g == SPREAD + 1:
                        slot_rows()
            fill_misc(LAST_USES[0])
            pv(B - 1, 3)
            for key in LAST_USES[1:]:
                fill_misc(key)


def kernel(**inputs):
    import numpy as np
    import concourse.bacc as bacc
    from concourse import mybir as _mybir
    from concourse.bass_utils import run_bass_kernel_spmd as run

    x = np.ascontiguousarray(inputs["L0_attn_x"])
    E = x.shape[-1]
    w = np.asarray(inputs["L0_attn_W1"]).reshape(E, 2, HEADS // 2, 3, E // HEADS)
    b = np.asarray(inputs["L0_attn_b1"]).reshape(2, HEADS // 2, 3, E // HEADS)
    arrays = {
        "x": x,
        "w_qk": w[:, :, :, 0:2].transpose(0, 3, 1, 4, 2).reshape(E, 2, E),
        "b_qk": b[:, :, 0:2].transpose(0, 3, 1, 2).reshape(E, 2),
        "w_v": w[:, :, :, 2].reshape(E, E),
        "b_v": b[:, :, 2].reshape(E),
        "w_p": np.asarray(inputs["L0_attn_Wp"]),
        "b_p": np.asarray(inputs["L0_attn_bp"]),
        "w_gate": np.asarray(inputs["L0_ffn_wg"]),
        "w1": np.asarray(inputs["L0_ffn_w1"]),
        "w3": np.asarray(inputs["L0_ffn_w3"]),
        "w2": np.asarray(inputs["L0_ffn_w2"]),
    }
    arrays = {k: np.ascontiguousarray(v) for k, v in arrays.items()}
    nc = bacc.Bacc("TRN2", target_bir_lowering=False, num_devices=1)
    args = [nc.dram_tensor(k, v.shape, _mybir.dt.from_np(v.dtype), kind="ExternalInput").ap()
            for k, v in arrays.items()]
    out = nc.dram_tensor("out", x.shape, _mybir.dt.from_np(x.dtype), kind="ExternalOutput").ap()
    attention_moe_block(nc, *args, out)
    r = run(nc, [arrays], core_ids=[0])
    return r.results[0]["out"]
```
